# Optimizing a Trainium2 kernel written in Bass

```python
import numpy as np
import jax
import jax.numpy as jnp

def _softmax(x, axis=-1):
    return jax.nn.softmax(x, axis=axis)

def _gelu(x):
    return jax.nn.gelu(x, approximate=True)

def _silu(x):
    return jax.nn.silu(x)

def _sigmoid(x):
    return jax.nn.sigmoid(x)

def _layernorm(x, axis=-1, eps=1e-05):
    m = jnp.mean(x, axis=axis, keepdims=True)
    v = jnp.var(x, axis=axis, keepdims=True)
    return (x - m) / jnp.sqrt(v + eps)

def _scatter_add(tgt, idx, src, axis=0):
    return tgt.at[idx].add(src)

def _segment_sum(src, seg, n):
    return jax.ops.segment_sum(src, seg, n)
kernel_name = 'mk_adaln_d1_jaxref_r8_8dbf39'

def setup_inputs(seed: int=0):
    np.random.seed(seed)
    _w = jnp.asarray

    def _L0_attn_setup():
        import jax, jax.numpy as jnp
        import numpy as np
        BATCH, L, D, N, K = (2, 256, 128, 32, 4)

        def _forward(x, in_proj_w, in_proj_b, conv_w, conv_b, A_log, B_w, B_b, C_w, C_b, dt_w, dt_b, out_w, out_b, ln_g, ln_beta):
            batch, seqlen, d = x.shape
            residual = x
            xz = x @ in_proj_w.T + in_proj_b
            xc, z = (xz[..., :d], xz[..., d:])
            xt = jnp.swapaxes(xc, 1, 2)
            conv = jax.lax.conv_general_dilated(xt, conv_w, window_strides=(1,), padding=[(2, 2)], feature_group_count=d, dimension_numbers=('NCH', 'OIH', 'NCH'))
            conv = conv + conv_b[None, :, None]
            xs = jax.nn.silu(jnp.swapaxes(conv, 1, 2)[:, :seqlen])
            A = -jnp.exp(jnp.clip(A_log, -5.0, 2.0))
            Bm = xs @ B_w.T + B_b
            Cm = xs @ C_w.T + C_b
            dt = jnp.clip(jax.nn.softplus(xs @ dt_w.T + dt_b), 0.001, 0.2)

            def step(state, inp):
                x_t, dt_t, B_t, C_t = inp
                A_bar = jnp.exp(dt_t[:, :, None] * A[None])
                B_bar = dt_t[:, :, None] * B_t[:, None, :]
                state = jnp.clip(state * A_bar + B_bar * x_t[:, :, None], -10.0, 10.0)
                y = jnp.einsum('bn,bdn->bd', C_t, state)
                return (state, y)
            init = jnp.zeros((batch, d, A.shape[1]), xs.dtype)
            seq = (jnp.swapaxes(xs, 0, 1), jnp.swapaxes(dt, 0, 1), jnp.swapaxes(Bm, 0, 1), jnp.swapaxes(Cm, 0, 1))
            _, ys = jax.lax.scan(step, init, seq)
            y = jnp.swapaxes(ys, 0, 1) * jax.nn.silu(z)
            out = y @ out_w.T + out_b + residual
            mu = out.mean(-1, keepdims=True)
            var = out.var(-1, keepdims=True)
            return ln_g * (out - mu) * jax.lax.rsqrt(var + 1e-05) + ln_beta
        key = jax.random.key(seed)
        ks = jax.random.split(key, 16)

        def nrm(k, shape, std=0.02, mean=0.0):
            return mean + std * jax.random.normal(k, shape, jnp.float32)
        lim = 1.0 / np.sqrt(D)
        return {'x': jax.random.normal(ks[0], (BATCH, L, D), jnp.float32), 'in_proj_w': jax.random.uniform(ks[1], (2 * D, D), jnp.float32, -lim, lim), 'in_proj_b': jax.random.uniform(ks[2], (2 * D,), jnp.float32, -lim, lim), 'conv_w': jax.random.uniform(ks[3], (D, 1, K), jnp.float32, -0.5, 0.5), 'conv_b': jax.random.uniform(ks[4], (D,), jnp.float32, -0.5, 0.5), 'A_log': nrm(ks[5], (D, N), std=0.1, mean=-2.0), 'B_w': nrm(ks[6], (N, D)), 'B_b': jnp.zeros((N,), jnp.float32), 'C_w': nrm(ks[7], (N, D)), 'C_b': jnp.zeros((N,), jnp.float32), 'dt_w': nrm(ks[8], (D, D)), 'dt_b': jnp.zeros((D,), jnp.float32), 'out_w': nrm(ks[9], (D, D)), 'out_b': jnp.zeros((D,), jnp.float32), 'ln_g': jnp.ones((D,), jnp.float32), 'ln_beta': jnp.zeros((D,), jnp.float32)}
    _L0_attn_in = _L0_attn_setup()

    def _L0_ffn_setup():
        import jax, jax.numpy as jnp
        import numpy as np
        B, T, D = (2, 128, 128)
        E = 16
        H = 256
        K = 2
        HS = H * 2
        key = jax.random.key(seed)
        ks = jax.random.split(key, 16)
        s = 0.02
        f32 = jnp.float32
        return {'x': jax.random.normal(ks[0], (B, T, D), f32), 'Wg': jax.random.normal(ks[1], (D, E), f32) * s, 'W1': jax.random.normal(ks[2], (E, D, H), f32) * s, 'b1': jax.random.normal(ks[3], (E, H), f32) * s, 'W11': jax.random.normal(ks[4], (E, D, H), f32) * s, 'b11': jax.random.normal(ks[5], (E, H), f32) * s, 'W2': jax.random.normal(ks[6], (E, H, D), f32) * s, 'b2': jax.random.normal(ks[7], (E, D), f32) * s, 'Ws1': jax.random.normal(ks[8], (D, HS), f32) * s, 'bs1': jax.random.normal(ks[9], (HS,), f32) * s, 'Ws11': jax.random.normal(ks[10], (D, HS), f32) * s, 'bs11': jax.random.normal(ks[11], (HS,), f32) * s, 'Ws2': jax.random.normal(ks[12], (HS, D), f32) * s, 'bs2': jax.random.normal(ks[13], (D,), f32) * s}
    _L0_ffn_in = _L0_ffn_setup()
    _L0_c = _w((lambda *s: np.random.randn(*s).astype(np.float32) * 0.05)(8, 128))
    _L0_wmod = _w((lambda *s: np.random.randn(*s).astype(np.float32) * 0.05)(128, 6 * 128) * 128 ** (-0.5))
    _d = {'L0_attn_x': _L0_attn_in['x'], 'L0_attn_in_proj_w': _L0_attn_in['in_proj_w'], 'L0_attn_in_proj_b': _L0_attn_in['in_proj_b'], 'L0_attn_conv_w': _L0_attn_in['conv_w'], 'L0_attn_conv_b': _L0_attn_in['conv_b'], 'L0_attn_A_log': _L0_attn_in['A_log'], 'L0_attn_B_w': _L0_attn_in['B_w'], 'L0_attn_B_b': _L0_attn_in['B_b'], 'L0_attn_C_w': _L0_attn_in['C_w'], 'L0_attn_C_b': _L0_attn_in['C_b'], 'L0_attn_dt_w': _L0_attn_in['dt_w'], 'L0_attn_dt_b': _L0_attn_in['dt_b'], 'L0_attn_out_w': _L0_attn_in['out_w'], 'L0_attn_out_b': _L0_attn_in['out_b'], 'L0_attn_ln_g': _L0_attn_in['ln_g'], 'L0_attn_ln_beta': _L0_attn_in['ln_beta'], 'L0_ffn_Wg': _L0_ffn_in['Wg'], 'L0_ffn_W1': _L0_ffn_in['W1'], 'L0_ffn_b1': _L0_ffn_in['b1'], 'L0_ffn_W11': _L0_ffn_in['W11'], 'L0_ffn_b11': _L0_ffn_in['b11'], 'L0_ffn_W2': _L0_ffn_in['W2'], 'L0_ffn_b2': _L0_ffn_in['b2'], 'L0_ffn_Ws1': _L0_ffn_in['Ws1'], 'L0_ffn_bs1': _L0_ffn_in['bs1'], 'L0_ffn_Ws11': _L0_ffn_in['Ws11'], 'L0_ffn_bs11': _L0_ffn_in['bs11'], 'L0_ffn_Ws2': _L0_ffn_in['Ws2'], 'L0_ffn_bs2': _L0_ffn_in['bs2'], 'L0_c': _L0_c, 'L0_wmod': _L0_wmod}
    _x0 = _d['L0_attn_x']
    _d['L0_attn_x'] = jax.random.normal(jax.random.fold_in(jax.random.key(seed), 1), (8, 512, 128), dtype=_x0.dtype)
    del _x0
    return _d

def reference(L0_attn_x, L0_attn_in_proj_w, L0_attn_in_proj_b, L0_attn_conv_w, L0_attn_conv_b, L0_attn_A_log, L0_attn_B_w, L0_attn_B_b, L0_attn_C_w, L0_attn_C_b, L0_attn_dt_w, L0_attn_dt_b, L0_attn_out_w, L0_attn_out_b, L0_attn_ln_g, L0_attn_ln_beta, L0_ffn_Wg, L0_ffn_W1, L0_ffn_b1, L0_ffn_W11, L0_ffn_b11, L0_ffn_W2, L0_ffn_b2, L0_ffn_Ws1, L0_ffn_bs1, L0_ffn_Ws11, L0_ffn_bs11, L0_ffn_Ws2, L0_ffn_bs2, L0_c, L0_wmod):

    def _L0_attn_ref(x, in_proj_w, in_proj_b, conv_w, conv_b, A_log, B_w, B_b, C_w, C_b, dt_w, dt_b, out_w, out_b, ln_g, ln_beta):
        import jax, jax.numpy as jnp
        import numpy as np
        BATCH, L, D, N, K = (2, 256, 128, 32, 4)

        def _forward(x, in_proj_w, in_proj_b, conv_w, conv_b, A_log, B_w, B_b, C_w, C_b, dt_w, dt_b, out_w, out_b, ln_g, ln_beta):
            batch, seqlen, d = x.shape
            residual = x
            xz = x @ in_proj_w.T + in_proj_b
            xc, z = (xz[..., :d], xz[..., d:])
            xt = jnp.swapaxes(xc, 1, 2)
            conv = jax.lax.conv_general_dilated(xt, conv_w, window_strides=(1,), padding=[(2, 2)], feature_group_count=d, dimension_numbers=('NCH', 'OIH', 'NCH'))
            conv = conv + conv_b[None, :, None]
            xs = jax.nn.silu(jnp.swapaxes(conv, 1, 2)[:, :seqlen])
            A = -jnp.exp(jnp.clip(A_log, -5.0, 2.0))
            Bm = xs @ B_w.T + B_b
            Cm = xs @ C_w.T + C_b
            dt = jnp.clip(jax.nn.softplus(xs @ dt_w.T + dt_b), 0.001, 0.2)

            def step(state, inp):
                x_t, dt_t, B_t, C_t = inp
                A_bar = jnp.exp(dt_t[:, :, None] * A[None])
                B_bar = dt_t[:, :, None] * B_t[:, None, :]
                state = jnp.clip(state * A_bar + B_bar * x_t[:, :, None], -10.0, 10.0)
                y = jnp.einsum('bn,bdn->bd', C_t, state)
                return (state, y)
            init = jnp.zeros((batch, d, A.shape[1]), xs.dtype)
            seq = (jnp.swapaxes(xs, 0, 1), jnp.swapaxes(dt, 0, 1), jnp.swapaxes(Bm, 0, 1), jnp.swapaxes(Cm, 0, 1))
            _, ys = jax.lax.scan(step, init, seq)
            y = jnp.swapaxes(ys, 0, 1) * jax.nn.silu(z)
            out = y @ out_w.T + out_b + residual
            mu = out.mean(-1, keepdims=True)
            var = out.var(-1, keepdims=True)
            return ln_g * (out - mu) * jax.lax.rsqrt(var + 1e-05) + ln_beta
        return _forward(x, in_proj_w, in_proj_b, conv_w, conv_b, A_log, B_w, B_b, C_w, C_b, dt_w, dt_b, out_w, out_b, ln_g, ln_beta)

    def _L0_ffn_ref(x, Wg, W1, b1, W11, b11, W2, b2, Ws1, bs1, Ws11, bs11, Ws2, bs2):
        import jax, jax.numpy as jnp
        import numpy as np
        B, T, D = (2, 128, 128)
        E = 16
        H = 256
        K = 2
        HS = H * 2
        b, t, d = x.shape
        xf = x.reshape(b * t, d)
        n = xf.shape[0]
        logits = xf @ Wg
        _, topi = jax.lax.top_k(logits, K)
        mask = jnp.zeros((n, E), bool).at[jnp.arange(n)[:, None], topi].set(True)
        gates = jax.nn.softmax(jnp.where(mask, logits, -jnp.inf), axis=-1)
        y = jnp.zeros_like(xf)
        for e in range(E):
            h = jax.nn.silu(xf @ W1[e] + b1[e]) * (xf @ W11[e] + b11[e])
            y = y + (h @ W2[e] + b2[e]) * gates[:, e, None]
        z = jax.nn.silu(xf @ Ws1 + bs1) * (xf @ Ws11 + bs11) @ Ws2 + bs2
        return (y + z).reshape(b, t, d)
    x = L0_attn_x
    mod = (_silu(L0_c) @ L0_wmod).reshape(L0_c.shape[0], 6, 1, -1)
    sa, ca, ga, sb, cb, gb = (mod[:, 0], mod[:, 1], mod[:, 2], mod[:, 3], mod[:, 4], mod[:, 5])
    ga = (2 * (ga >= 0) - 1) * jnp.maximum(jnp.abs(ga), 0.25)
    gb = (2 * (gb >= 0) - 1) * jnp.maximum(jnp.abs(gb), 0.25)
    h = _layernorm(x, axis=-1) * (1 + ca) + sa
    x = x + ga * _L0_attn_ref(h, L0_attn_in_proj_w, L0_attn_in_proj_b, L0_attn_conv_w, L0_attn_conv_b, L0_attn_A_log, L0_attn_B_w, L0_attn_B_b, L0_attn_C_w, L0_attn_C_b, L0_attn_dt_w, L0_attn_dt_b, L0_attn_out_w, L0_attn_out_b, L0_attn_ln_g, L0_attn_ln_beta)
    h = _layernorm(x, axis=-1) * (1 + cb) + sb
    x = x + gb * _L0_ffn_ref(h, L0_ffn_Wg, L0_ffn_W1, L0_ffn_b1, L0_ffn_W11, L0_ffn_b11, L0_ffn_W2, L0_ffn_b2, L0_ffn_Ws1, L0_ffn_bs1, L0_ffn_Ws11, L0_ffn_bs11, L0_ffn_Ws2, L0_ffn_bs2)
    return x

_drawn_inputs = setup_inputs


def setup_inputs(seed=0):
    import zlib

    import numpy as np

    out = dict(_drawn_inputs(seed))
    spreads = {'L0_attn_B_b': (0.0, 0.8),
     'L0_attn_C_b': (0.0, 0.8),
     'L0_attn_dt_b': (0.0, 0.1),
     'L0_attn_out_b': (0.0, 2.0),
     'L0_attn_ln_g': (1.0, 0.2),
     'L0_attn_ln_beta': (0.0, 0.307)}
    factors = {'L0_attn_in_proj_w': 8.0,
     'L0_attn_in_proj_b': 8.0,
     'L0_attn_conv_w': 8.0,
     'L0_attn_conv_b': 8.0,
     'L0_attn_A_log': 8.0,
     'L0_attn_B_w': 8.0,
     'L0_attn_C_w': 8.0,
     'L0_attn_out_w': 8.0,
     'L0_ffn_Wg': 8.0,
     'L0_ffn_W1': 8.0,
     'L0_ffn_b1': 8.0,
     'L0_ffn_W11': 8.0,
     'L0_ffn_b11': 8.0,
     'L0_ffn_W2': 8.0,
     'L0_ffn_b2': 35.622,
     'L0_ffn_Ws1': 8.0,
     'L0_ffn_bs1': 8.0,
     'L0_ffn_Ws11': 8.0,
     'L0_ffn_bs11': 8.0,
     'L0_ffn_Ws2': 8.0,
     'L0_ffn_bs2': 27.036}
    for name, (base, spread) in spreads.items():
        noise = np.random.default_rng([zlib.crc32(name.encode()), seed]).standard_normal(out[name].shape)
        drawn = base * np.exp(spread * noise) if base else spread * noise
        out[name] = jnp.asarray(drawn.astype(out[name].dtype))
    for name, factor in factors.items():
        out[name] = (out[name] * factor).astype(out[name].dtype)
    return out
```

```python
from contextlib import ExitStack

import concourse.bass as bass
from concourse import mybir

F32 = mybir.dt.float32
BF16 = mybir.dt.bfloat16
ALU = mybir.AluOpType
ACT = mybir.ActivationFunctionType
AX = mybir.AxisListType

B, T, D, N = 8, 512, 128, 32
E, H, HS = 16, 256, 512
P = 128
TT = P // B
TC = 64
NC = T // TC
CT = TC // TT
CW = TC * B
HB = B // 2
GT = 8
NG = T // GT
PARTS = 3
ROWS = PARTS * HB
SW = 2 * D
GW = 2 * GT * SW
SHARED = HS // H
NE = SHARED + E
MH = H // P
PER = 4
PAIRS = 2 * PER
BODIES = E // PER
EPS = 1e-5
XPAD = 2
KW = 4
INIT = 1
STORES = CT * PARTS * TT // GT


class Chain:

    def __init__(self, eng, sem):
        self.eng, self.sem, self.base, self.n = eng, sem, 0, 0

    def at(self, base):
        self.base, self.n = base, 0

    def __call__(self, ins):
        ins.then_inc(self.sem, 1)
        self.n += 1

    def wait(self):
        self.eng.wait_ge(self.sem, self.base + self.n)


def build(nc, x, wcol, wmod, w1, w2, b2, out):
    with ExitStack() as ctx:
        def sb(name, cols, dt=F32, parts=P):
            return ctx.enter_context(nc.sbuf_tensor(name, [parts, cols], dt))

        def bank(name):
            return ctx.enter_context(nc.psum_tensor(name, [P, 512], F32))

        def sem(name):
            return ctx.enter_context(nc.semaphore(name))

        names = dict(win=2 * D, wdt=D, wb=N, wc=N, wout=D, wg=E, arep=D, ident=D, ct=P, cols=16,
                     dtb=D, outb=D, lng=D, lnb=D, sel=P, order=E)
        at, o = {}, 0
        for k, v in names.items():
            at[k] = (o, o + v)
            o += v
        wc_sb = sb("wc_sb", o)

        def cst(name):
            a, b = at[name]
            return wc_sb[:, a:b]

        c0 = at["cols"][0]

        def col(i):
            return wc_sb[:, c0 + i:c0 + i + 1]

        IN_B, CONV_W, CONV_B, B_B, C_B, BS2, ONE = 0, 2, 6, 7, 8, 9, 10
        wmod_sb = sb("wmod_sb", 6 * D)
        sct = sb("sct", P)
        sel_bf = sb("sel_bf", P, BF16, ROWS)
        b2_sb = sb("b2_sb", D, F32, E)
        mods = sb("mods", 6 * D)
        SA, CA, GA, SB, CB, GB = (mods[:, i * D:(i + 1) * D] for i in range(6))
        gmag = sb("gmag", 2 * D)
        gsgn = sb("gsgn", 2 * D)
        arep = sb("arep", D)
        gg = sb("gg", D)
        gbias = sb("gbias", D)
        mexp = sb("mexp", CT)
        half_gate = sb("half_gate", CW)

        X = sb("X", T * B * D // P)
        HR = sb("HR", T * B * D // P)
        ZG = sb("ZG", T * B)
        XC = sb("XC", (T + KW - 1) * B)
        XS = sb("XS", T * B)
        BCOL = sb("BCOL", 2 * (T + GT))
        BNOW = [sb(f"BNOW{i}", 2 * GT) for i in range(2)]
        CBLK = sb("CBLK", T * B)

        st = sb("st", CT * 6)
        mean, mdif, vsum = (sb(n, CT) for n in ("mean", "mdif", "vsum"))
        vareps = sb("vareps", CT)
        rstd = sb("rstd", CT)
        Hn = [sb(f"Hn{i}", CW) for i in range(2)]
        hT = [sb(f"hT{i}", CW) for i in range(2)]
        dti = sb("dti", CW)
        dte = sb("dte", CW)
        dtl = sb("dtl", CW)
        DU = [sb(f"DU{i}", 2 * CW) for i in range(2)]
        res1 = sb("res1", 2 * CW)
        res2 = sb("res2", 2 * CW)
        PB = [sb(f"PB{i}", PARTS * 2 * CW, BF16) for i in range(2)]
        R = [sb(f"R{i}", GW, BF16, ROWS) for i in range(2)]
        dtc = [sb(f"dtc{i}", 2 * SW) for i in range(2)]
        dta = [sb(f"dta{i}", 2 * SW) for i in range(2)]
        ab = [sb(f"ab{i}", 2 * SW) for i in range(2)]
        SR = 8
        S = [sb(f"S{i}", SW) for i in range(SR)]
        pt = sb("pt", SW)
        qt = sb("qt", SW)
        W1S = [sb(f"W1S{i}", 2 * H + 2 * MH) for i in range(2)]
        W2S = [sb(f"W2S{i}", MH * D) for i in range(2)]
        GS = [dti, dte]
        hid = [t[:, i * MH * CW:(i + 1) * MH * CW] for t in (XS, XC) for i in range(4)]
        hb, th1, m0, th, wg_ = hid[0:2], hid[2:4], hid[4:6], hid[6], hid[7]
        hh = DU
        ygT = hT[0]
        om, X2, O = res1[:, 0:CW], res1[:, CW:2 * CW], res2[:, 0:CW]
        h2T = hT[1]
        lg = sb("lg", CT * E)
        top, top2, place = (sb(n, CT) for n in ("top", "top2", "place"))
        pick1, pick2 = (sb(n, CT * E) for n in ("pick1", "pick2"))
        rp = sb("rp", CT * E)
        ex = sb("ex", CT * E)
        gsum = sb("gsum", CT)
        grec = sb("grec", CT)
        gt = sb("gt", CT * E)
        gT, yT = dtl[0:E, :], res2[:, CW:2 * CW]

        YACC, YSC, DTB, U0, U1, HA, HBk, HC = (
            bank(n) for n in ("YACC", "YSC", "DTB", "U0", "U1", "HA", "HBk", "HC"))
        U = [U0, U1]

        DS = nc.dram_tensor("scan_rows", ((NG + 2) * ROWS, GW), BF16).ap()
        GD = nc.dram_tensor("gate_rows", (NE, CW), F32).ap()

        ld_x, ld_w = sem("ld_x"), sem("ld_w")
        dve_own = sem("dve_own")
        pool_const = sem("pool_const")
        sct_ready, mod_ps, mod_ready = sem("sct_ready"), sem("mod_ps"), sem("mod_ready")
        var_ready, rstd_ready = sem("var_ready"), sem("rstd_ready")
        h_ready, hr_done, xg_done = sem("h_ready"), sem("hr_done"), sem("xg_done")
        hT_ps, hT_ready, inp_ps, xc_ready, z_ready = (
            sem(n) for n in ("hT_ps", "hT_ready", "inp_ps", "xc_ready", "z_ready"))
        conv_done, xs_ready, bc_ps, bcol_ready = (
            sem(n) for n in ("conv_done", "xs_ready", "bc_ps", "bcol_ready"))
        xst_ready, dt_ps, dti_ready, dte_ready, dtl_ready, du_ready = (
            sem(n) for n in ("xst_ready", "dt_ps", "dti_ready", "dte_ready", "dtl_ready", "du_ready"))
        part_ready = [sem(f"part_ready{i}") for i in range(2)]
        ds_stored = [sem(f"ds_stored{i}") for i in range(2)]
        res_ready = sem("res_ready")
        r_loaded = [sem(f"r_loaded{i}") for i in range(2)]
        dt_bc, u_bc, dtc_ready, dta_ready, a_ready = (
            sem(n) for n in ("dt_bc", "u_bc", "dtc_ready", "dta_ready", "a_ready"))
        b_ready = sem("b_ready")
        p_done, q_done, s_done, y_done = (sem(n) for n in ("p_done", "q_done", "s_done", "y_done"))
        w1_loaded = [sem(f"w1_loaded{i}") for i in range(2)]
        w2_loaded = [sem(f"w2_loaded{i}") for i in range(2)]
        g_loaded = [sem(f"g_loaded{i}") for i in range(2)]
        h1_ps, h11_ps, hb_ready, th_ready, th1_ready = (
            sem(n) for n in ("h1_ps", "h11_ps", "hb_ready", "th_ready", "th1_ready"))
        m0_ready, wg_ready, hh_ready, w2_done = (
            sem(n) for n in ("m0_ready", "wg_ready", "hh_ready", "w2_done"))
        yg_ready, o_ps, h2_ready, h2T_ps, h2T_ready, lg_ps = (
            sem(n) for n in ("yg_ready", "o_ps", "h2_ready", "h2T_ps", "h2T_ready", "lg_ps"))
        lgd_ready, ex_ready, gt_ready, gT_ps, gT_ready, gd_stored = (
            sem(n) for n in ("lgd_ready", "ex_ready", "gt_ready", "gT_ps", "gT_ready", "gd_stored"))
        const_ready, aexp_ready, arep_ready = sem("const_ready"), sem("aexp_ready"), sem("arep_ready")
        zero_rows, gate_ones, yacc_ps, dt_clipped = (
            sem(n) for n in ("zero_rows", "gate_ones", "yacc_ps", "dt_clipped"))
        yT_ready, yt_ps, out_ready, stored = (
            sem(n) for n in ("yT_ready", "yt_ps", "out_ready", "stored"))

        def tiles(ap, w=D):
            return ap.rearrange("p (j d) -> p j d", d=w)

        def over_tiles(ap, n=CT):
            return ap.unsqueeze(1).broadcast_to([P, n, D])

        block = ctx.enter_context(nc.Block())

        @block.sync
        def _(sp):
            for x_stored in (*ds_stored, stored):
                sp.sem_inc(x_stored, 16 * INIT)
            sp.dma_start(wc_sb[:, :], wcol).then_inc(ld_w, 16)
            sp.dma_start(wmod_sb[:, :], wmod).then_inc(ld_w, 16)
            sp.dma_start(b2_sb[:, :], b2).then_inc(ld_w, 16)
            sp.dma_start(X[:, :], x).then_inc(ld_x, 16)

            sp.wait_ge(pool_const, 3)
            zeros = S[0][0:ROWS, :].bitcast(BF16)
            for g in range(NG, NG + 2):
                for c in range(8):
                    sp.dma_start(DS[g * ROWS:(g + 1) * ROWS, c * GW // 8:(c + 1) * GW // 8], zeros
                                 ).then_inc(zero_rows, 16)
            dv = DS.rearrange("(g m b) (q t h d) -> g m t h b q d", m=PARTS, b=HB, q=2, h=2, d=D)
            with sp.Fori(0, NC // 2) as c2:
                for u in range(2):
                    sp.wait_ge(part_ready[u], (c2 + 1) * PARTS + INIT)
                    src = PB[u][:, :].rearrange("p (m q j d) -> p m q j d", m=PARTS, q=2, d=D)
                    for j in range(CT):
                        for m in range(PARTS):
                            for tg in range(TT // GT):
                                g = c2 * (2 * CT * TT // GT) + (u * CT + j) * (TT // GT) + tg
                                sp.dma_start(
                                    dv[bass.ds(g, 1), m].rearrange("g t h b q d -> (g t h) b q d"),
                                    src[64 * tg:64 * tg + 64, m, :, j, :]).then_inc(ds_stored[u], 16)
            sp.wait_ge(zero_rows, 16 * 16)
            for u in range(2):
                sp.wait_ge(ds_stored[u], STORES * (NC // 2) * 16 + 16 * INIT)

            def load_rows(g, slot):
                sp.dma_start(R[slot][:, :], DS[bass.ds(g * ROWS, ROWS), :]).then_inc(r_loaded[slot], 16)

            def load_expert(dst, src, k, loaded):
                sp.dma_start(dst[:, :], src[bass.ds(k, 1)].rearrange("a p f -> (a p) f")).then_inc(loaded, 16)

            def load_gate(k, slot):
                sp.dma_start(GS[slot][:, :], GD[bass.ds(k, 1), :].broadcast_to([P, CW])
                             ).then_inc(g_loaded[slot], 16)

            load_rows(0, 0)
            load_rows(1, 1)
            sp.wait_ge(pool_const, 5)
            sp.dma_start(GD[0:SHARED, :], half_gate[0:SHARED, :]).then_inc(gd_stored, 16)

            def stage(s, scan, ffn):
                q = s - 1
                if ffn:
                    for k in range(SHARED):
                        load_expert(W1S[k], w1, k, w1_loaded[k])
                        load_expert(W2S[k], w2, k, w2_loaded[k])
                    sp.wait_ge(gT_ready, s)
                    sp.dma_start(GD[SHARED:NE, :], gT[:, :]).then_inc(gd_stored, 16)
                    sp.wait_ge(gd_stored, s * 16 + 16)
                    for k in range(SHARED):
                        load_gate(k, k)
                with sp.Fori(0, BODIES) as i:
                    for j in range(PER):
                        if ffn:
                            k = i * PER + j + SHARED
                            kk = q * NE + k
                            slot = j % 2
                            sp.wait_ge(m0_ready, (kk - 1) * MH + INIT)
                            load_expert(W1S[slot], w1, k, w1_loaded[slot])
                            sp.wait_ge(wg_ready, kk - 1)
                            load_gate(k, slot)
                            sp.wait_ge(w2_done, kk - 1)
                            load_expert(W2S[slot], w2, k, w2_loaded[slot])
                        if scan and j % 2:
                            g = s * (TC // GT) + i * 2 + j // 2
                            sp.wait_ge(u_bc, g * (GT // 2) + GT // 2)
                            sp.wait_ge(dt_bc, g * (GT // 2) + GT // 2)
                            load_rows(g + 2, j // 2)
                if ffn:
                    sp.wait_ge(out_ready, s)
                    sp.dma_start(out[:, bass.ds(q * CW, CW)], O[:, :]).then_inc(stored, 16)

            stage(0, True, False)
            with sp.Fori(1, NC) as s:
                stage(s, True, True)
            stage(NC, False, True)
            sp.wait_ge(stored, 16 * NC + 16 * INIT)
            for r in r_loaded:
                sp.wait_ge(r, (1 + NC * BODIES) * 16)

        @block.gpsimd
        def _(pool):
            for started in (hr_done, hh_ready):
                pool.sem_inc(started, INIT)
            nc.gpsimd.memset(S[0][:, :], 0.0).then_inc(pool_const, 1)
            nc.gpsimd.memset(CBLK[:, :], 0.0).then_inc(pool_const, 1)
            nc.gpsimd.memset(XC[:, :], 0.0).then_inc(pool_const, 1)
            nc.gpsimd.memset(mexp[:, :], -0.5).then_inc(pool_const, 1)
            nc.gpsimd.memset(half_gate[:, :], 0.5).then_inc(pool_const, 1)
            pool.wait_ge(pool_const, 5)

            def inv_std(n):
                pool.wait_ge(var_ready, n + 1)
                nc.gpsimd.tensor_tensor(rstd[:, :], vareps[:, :], mexp[:, :], ALU.pow).then_inc(rstd_ready, 1)

            with pool.Fori(0, NC // 2) as c2:
                for u in range(2):
                    c = c2 * 2 + u
                    inv_std(c)
                    pool.wait_ge(h_ready, c + 1)
                    cols = bass.ds(c2 * (2 * CW) + u * CW, CW)
                    nc.gpsimd.tensor_tensor(tiles(HR[:, cols]), tiles(Hn[u][:, :]), over_tiles(cst("outb")),
                                            ALU.add).then_inc(hr_done, 1)
                    nc.gpsimd.tensor_tensor(tiles(X[:, cols]), tiles(X[:, cols]), over_tiles(gbias[:, :]),
                                            ALU.add).then_inc(xg_done, 1)

            with pool.Fori(0, NC // 2) as c2:
                for u in range(2):
                    c = c2 * 2 + u
                    part = PB[u][:, :].rearrange("p (m f) -> p m f", m=PARTS)
                    pool.wait_ge(part_ready[u], c2 * PARTS + 1 + INIT)
                    nc.gpsimd.tensor_tensor(res1[:, :], DU[u][:, :], part[:, 0, :], ALU.subtract
                                            ).then_inc(res_ready, 1)
                    pool.wait_ge(part_ready[u], c2 * PARTS + 2 + INIT)
                    pool.wait_ge(res_ready, c * 2 + 1)
                    nc.gpsimd.tensor_tensor(res2[:, :], res1[:, :], part[:, 1, :], ALU.subtract
                                            ).then_inc(res_ready, 1)

            def dt_times_a(p, slot):
                pool.wait_ge(dtc_ready, p + 1)
                nc.gpsimd.tensor_tensor(tiles(dta[slot][:, :]), tiles(dtc[slot][:, :]), over_tiles(arep[:, :]),
                                        ALU.mult).then_inc(dta_ready, 1)

            def gated(kk, slot):
                pool.wait_ge(th1_ready, kk + 1 + INIT)
                pool.wait_ge(hh_ready, kk + INIT)
                nc.gpsimd.tensor_tensor(wg_[:, :].rearrange("p (m f) -> p m f", m=MH),
                                        th1[slot][:, :].rearrange("p (m f) -> p m f", m=MH),
                                        GS[slot][:, :].unsqueeze(1).broadcast_to([P, MH, CW]), ALU.mult
                                        ).then_inc(wg_ready, 1)

            def hidden(kk, slot):
                pool.wait_ge(m0_ready, (kk + 1) * MH + INIT)
                pool.wait_ge(wg_ready, kk + 1)
                nc.gpsimd.tensor_tensor(hh[slot][:, :], m0[slot][:, :], wg_[:, :], ALU.mult
                                        ).then_inc(hh_ready, 1)

            pool.wait_ge(arep_ready, 1)
            dt_times_a(0, 0)
            dt_times_a(1, 1)

            def stage(s, scan, ffn):
                q = s - 1

                def expert(kk, n, slot, prev, p):
                    if prev:
                        pool.wait_ge(g_loaded[1 - slot], n * 16)
                        gated(kk - 1, 1 - slot)
                    if p is not None:
                        pool.wait_ge(a_ready, p + 1)
                        dt_times_a(p + 2, 0)
                    if prev:
                        hidden(kk - 1, 1 - slot)
                    if p is not None:
                        pool.wait_ge(a_ready, p + 2)
                        dt_times_a(p + 3, 1)

                if ffn:
                    inv_std(q * 2 + NC)
                    inv_std(q * 2 + (NC + 1))
                    expert(q * NE + 1, q * (NE // 2) + 1, 1, True, None)
                with pool.Fori(0, BODIES) as i:
                    for j in range(PER):
                        p = s * (TC // 2) + i * PAIRS + 2 * j
                        kk = q * NE + i * PER + (j + SHARED)
                        n = q * (NE // 2) + i * 2 + (1 + (j + 1) // 2)
                        expert(kk, n, j % 2, ffn, p if scan else None)
                if ffn:
                    expert(q * NE + NE, q * (NE // 2) + NE // 2, 0, True, None)

            stage(0, True, False)
            with pool.Fori(1, NC) as s:
                stage(s, True, True)
            stage(NC, False, True)

        @block.tensor
        def _(pe):
            pe.sem_inc(hT_ps, INIT)
            pe.sem_inc(y_done, SR)
            pe.wait_ge(ld_w, 48)
            pe.wait_ge(sct_ready, 1)
            nc.tensor.matmul(HA[:, 0:3 * D], sct[:, :], wmod_sb[:, 0:3 * D], start=True, stop=True)
            nc.tensor.matmul(HBk[:, 0:3 * D], sct[:, :], wmod_sb[:, 3 * D:6 * D], start=True, stop=True
                             ).then_inc(mod_ps, 1)
            pe.wait_ge(mod_ready, 1)
            ident = cst("ident")

            with pe.Fori(0, NC // 2) as c2:
                for u in range(2):
                    c = c2 * 2 + u
                    pe.wait_ge(h_ready, c + 1)
                    pe.wait_ge(hT_ready, c + INIT)
                    for j in range(CT):
                        mm = nc.tensor.transpose(HA[:, j * D:(j + 1) * D], Hn[u][:, j * D:(j + 1) * D], ident)
                    mm.then_inc(hT_ps, 1)
                    pe.wait_ge(hT_ready, c + 1 + INIT)
                    pe.wait_ge(z_ready, c + INIT)
                    nc.tensor.matmul(HBk[:, :], cst("win")[:, 0:D], hT[u][:, :], start=True, stop=True
                                     ).then_inc(inp_ps, 1)
                    nc.tensor.matmul(HC[:, :], cst("win")[:, D:2 * D], hT[u][:, :], start=True, stop=True
                                     ).then_inc(inp_ps, 1)

            pe.wait_ge(xs_ready, 2)
            xs3 = XS[:, :].rearrange("p (t b) -> p t b", b=B)
            for w, banks in (("wb", (HA, HBk)), ("wc", (HC, DTB))):
                for b in range(B):
                    mm = nc.tensor.matmul(banks[b // HB][N * (b % HB):N * (b % HB) + N, :], cst(w),
                                          xs3[:, :, b], start=True, stop=True)
            mm.then_inc(bc_ps, 1)

            with pe.Fori(0, NC // 2) as c2:
                for u in range(2):
                    c = c2 * 2 + u
                    pe.wait_ge(xst_ready, c + 1)
                    pe.wait_ge(du_ready, c + INIT)
                    for j in range(CT):
                        nc.tensor.matmul(U0[:, j * D:(j + 1) * D], hT[u][:, j * D:(j + 1) * D], cst("wdt"),
                                         start=True, stop=True)
                    for j in range(CT):
                        mm = nc.tensor.transpose(U1[:, j * D:(j + 1) * D], hT[u][:, j * D:(j + 1) * D], ident)
                    mm.then_inc(dt_ps, 1)

            def spread(bnk, n, what, ready):
                c = what * GW // 2 + n % 4 * 2 * SW
                nc.tensor.matmul(bnk[:, :], sel_bf[:, :], R[n // 4 % 2][:, c:c + 2 * SW], start=True, stop=True
                                 ).then_inc(ready, 1)

            pe.wait_ge(du_ready, NC + INIT)
            pe.wait_ge(bcol_ready, 1)
            pe.wait_ge(r_loaded[0], 16)
            spread(U[0], 0, 1, u_bc)
            spread(DTB, 0, 0, dt_bc)
            pe.wait_ge(dtc_ready, 1)
            spread(DTB, 1, 0, dt_bc)

            def stage(s, scan, ffn):
                q = s - 1

                def readout(i, n):
                    for h in range(2):
                        tl = i * (2 * PAIRS) + (2 * n + h)
                        pe.wait_ge(s_done, s * TC + tl + 1 + INIT)
                        for half in range(2):
                            mm = nc.tensor.matmul(
                                YSC[:, bass.ds(tl * B + half * HB, HB)],
                                S[(2 * n + h) % SR][:, half * D:(half + 1) * D],
                                CBLK[:, bass.ds((s * TC + tl) * B + half * HB, HB)], start=True, stop=True)
                        mm.then_inc(y_done, 1)

                def pair(i, n):
                    p = s * (TC // 2) + i * PAIRS + n
                    body = s * BODIES + i
                    if n:
                        readout(i, n - 1)
                    if (n + 1) % 4 == 0:
                        pe.wait_ge(r_loaded[(n + 1) // 4 % 2], (body + 1 + (n + 1) // 8) * 16)
                    pe.wait_ge(q_done, p * 4 + INIT)
                    spread(U[(n + 1) % 2], n + 1, 1, u_bc)
                    if (n + 2) % 4 == 0:
                        pe.wait_ge(r_loaded[(n + 2) // 4 % 2], (body + 1 + (n + 2) // 8) * 16)
                    pe.wait_ge(dtc_ready, p + 2)
                    spread(DTB, n + 2, 0, dt_bc)

                def second(kk, n, slot, first, last):
                    pe.wait_ge(hh_ready, kk + 1 + INIT)
                    pe.wait_ge(w2_loaded[slot], n * 16)
                    for m in range(MH):
                        mm = nc.tensor.matmul(YACC[:, :], W2S[slot][:, m * D:(m + 1) * D],
                                              hh[slot][:, m * CW:(m + 1) * CW],
                                              start=(first and m == 0), stop=False, skip_group_check=True)
                    mm.then_inc(w2_done, 1)

                def expert(kk, n, slot, prev, prev_first, i, pr):
                    w = W1S[slot]
                    if ffn:
                        pe.wait_ge(w1_loaded[slot], n * 16)
                        pe.wait_ge(hb_ready, kk * MH + INIT)
                        nc.tensor.matmul(HA[:, :], w[:, 0:D], h2T[:, :], start=True, stop=True
                                         ).then_inc(h1_ps, 1)
                        pe.wait_ge(m0_ready, kk * MH + INIT)
                        nc.tensor.matmul(HBk[:, :], w[:, H:H + D], h2T[:, :], start=True, stop=True
                                         ).then_inc(h11_ps, 1)
                    if pr is not None:
                        pair(i, pr)
                    if ffn:
                        pe.wait_ge(hb_ready, kk * MH + 1 + INIT)
                        nc.tensor.matmul(HA[:, :], w[:, D:2 * D], h2T[:, :], start=True, stop=True
                                         ).then_inc(h1_ps, 1)
                        nc.tensor.matmul(HC[:, :], w[:, H + D:H + 2 * D], h2T[:, :], start=True, stop=True
                                         ).then_inc(h11_ps, 1)
                    if pr is not None:
                        pair(i, pr + 1)
                    if prev:
                        second(kk - 1, n - 1 + slot, 1 - slot, prev_first, False)

                if ffn:
                    pe.wait_ge(yg_ready, s)
                    for j in range(CT):
                        mm = nc.tensor.matmul(HA[:, j * D:(j + 1) * D], ygT[:, j * D:(j + 1) * D], cst("wout"),
                                              start=True, stop=True)
                    mm.then_inc(o_ps, 1)
                    pe.wait_ge(h2_ready, s)
                    for j in range(CT):
                        mm = nc.tensor.transpose(HBk[:, j * D:(j + 1) * D], Hn[0][:, j * D:(j + 1) * D], ident)
                    mm.then_inc(h2T_ps, 1)
                    pe.wait_ge(h2T_ready, s)
                    for j in range(CT):
                        mm = nc.tensor.matmul(HC[:, j * E:(j + 1) * E], h2T[:, j * D:(j + 1) * D], cst("wg"),
                                              start=True, stop=True)
                    mm.then_inc(lg_ps, 1)
                    pe.wait_ge(gt_ready, s)
                    for j in range(CT):
                        mm = nc.tensor.transpose(HA[0:E, j * D:(j + 1) * D], gt[:, j * E:(j + 1) * E], ident)
                    mm.then_inc(gT_ps, 1)
                    pe.wait_ge(gT_ready, s)
                    expert(q * NE, q * (NE // 2) + 1, 0, False, False, 0, None)
                    expert(q * NE + 1, q * (NE // 2) + 1, 1, True, True, 0, None)
                with pe.Fori(0, BODIES) as i:
                    for j in range(PER):
                        expert(q * NE + i * PER + (j + SHARED), q * (NE // 2) + i * 2 + (2 + j // 2), j % 2,
                               ffn, False, i, 2 * j if scan else None)
                    if scan:
                        readout(i, PAIRS - 1)
                if ffn:
                    second(q * NE + (NE - 1), q * (NE // 2) + NE // 2, 1, False, False)
                    nc.tensor.matmul(YACC[:, :], b2_sb[:, :], gT[:, :], start=False, stop=True,
                                     skip_group_check=True).then_inc(yacc_ps, 1)
                    pe.wait_ge(yT_ready, s)
                    for j in range(CT):
                        mm = nc.tensor.transpose(HBk[:, j * D:(j + 1) * D], yT[:, j * D:(j + 1) * D], ident)
                    mm.then_inc(yt_ps, 1)

            stage(0, True, False)
            with pe.Fori(1, NC) as s:
                stage(s, True, True)
            stage(NC, False, True)

        @block.scalar
        def _(act):
            for started in (hT_ready, z_ready, hb_ready, th1_ready, dte_ready, *part_ready):
                act.sem_inc(started, INIT)
            act.wait_ge(ld_w, 48)
            nc.scalar.activation(sct[:, :], cst("ct"), ACT.Silu).then_inc(sct_ready, 1)

            with act.Fori(0, NC // 2) as c2:
                for u in range(2):
                    c = c2 * 2 + u
                    act.wait_ge(hT_ps, c + 1 + INIT)
                    nc.scalar.copy(hT[u][:, :], HA[:, :]).then_inc(hT_ready, 1)
                    act.wait_ge(inp_ps, c * 2 + 1)
                    if u == 0:
                        act.wait_ge(pool_const, 5)
                    nc.scalar.activation(XC[:, bass.ds(c * CW + XPAD * B, CW)], HBk[:, :], ACT.Identity,
                                         bias=col(IN_B)).then_inc(xc_ready, 1)
                    act.wait_ge(inp_ps, c * 2 + 2)
                    nc.scalar.activation(ZG[:, bass.ds(c * CW, CW)], HC[:, :], ACT.Silu,
                                         bias=col(IN_B + 1)).then_inc(z_ready, 1)
            for h in range(2):
                v = XS[:, h * T * B // 2:(h + 1) * T * B // 2]
                act.wait_ge(conv_done, h + 1)
                nc.scalar.activation(v, v, ACT.Silu).then_inc(xs_ready, 1)

            act.wait_ge(bc_ps, 1)
            for half, bnk in enumerate((HA, HBk)):
                nc.scalar.activation(BCOL[:, half * (T + GT):half * (T + GT) + T], bnk[:, :], ACT.Identity, bias=col(B_B))
            cv = CBLK[:, :].rearrange("p (t h b) -> p t h b", h=2, b=HB)
            for half, bnk in enumerate((HC, DTB)):
                for b in range(HB):
                    r = slice(N * b, N * b + N)
                    last = nc.scalar.activation(cv[r, :, half, b], bnk[r, :], ACT.Identity,
                                                bias=wc_sb[r, c0 + C_B:c0 + C_B + 1])
            last.then_inc(bcol_ready, 1)

            act.wait_ge(const_ready, 1)
            nc.scalar.activation(arep[:, :], arep[:, :], ACT.Exp).then_inc(aexp_ready, 1)
            with act.Fori(0, NC // 2) as c2:
                for u in range(2):
                    c = c2 * 2 + u
                    nc.scalar.copy(hT[u][:, :], XS[:, bass.ds(c * CW, CW)]).then_inc(xst_ready, 1)
                    act.wait_ge(dti_ready, c + 1)
                    nc.scalar.activation(dte[:, :], dti[:, :], ACT.Exp).then_inc(dte_ready, 1)
                    act.wait_ge(dte_ready, c + 1 + INIT)
                    nc.scalar.activation(dtl[:, :], dte[:, :], ACT.Ln, bias=col(ONE)).then_inc(dtl_ready, 1)
                    part = PB[u][:, :].rearrange("p (m f) -> p m f", m=PARTS)
                    act.wait_ge(du_ready, c + 1 + INIT)
                    act.wait_ge(ds_stored[u], c2 * (STORES * 16) + 16 * INIT)
                    nc.scalar.copy(part[:, 0, :], DU[u][:, :]).then_inc(part_ready[u], 1)
                    act.wait_ge(res_ready, c * 2 + 1)
                    nc.scalar.copy(part[:, 1, :], res1[:, :]).then_inc(part_ready[u], 1)
                    act.wait_ge(res_ready, c * 2 + 2)
                    nc.scalar.copy(part[:, 2, :], res2[:, :]).then_inc(part_ready[u], 1)

            def copy_dt(p, slot):
                act.wait_ge(dt_bc, p + 1)
                nc.scalar.copy(dtc[slot][:, :], DTB[:, :]).then_inc(dtc_ready, 1)

            def exp_dta(p, slot):
                act.wait_ge(dta_ready, p + 1)
                nc.scalar.activation(ab[slot][:, :], dta[slot][:, :], ACT.Exp).then_inc(a_ready, 1)

            copy_dt(0, 0)
            copy_dt(1, 1)
            exp_dta(0, 0)

            def stage(s, scan, ffn):
                q = s - 1

                def pair(i, n):
                    p = s * (TC // 2) + i * PAIRS + n
                    act.wait_ge(dta_ready, p + 1)
                    copy_dt(p + 2, n % 2)
                    act.wait_ge(p_done, p * 2 + INIT)
                    exp_dta(p + 1, (n + 1) % 2)

                def expert(kk, slot, i, pr):
                    w = W1S[slot]

                    def pre(m):
                        act.wait_ge(h1_ps, kk * MH + (m + 1))
                        nc.scalar.activation(hb[slot][:, m * CW:(m + 1) * CW], HA[:, :], ACT.Identity,
                                             bias=w[:, 2 * H + m:2 * H + m + 1]).then_inc(hb_ready, 1)

                    if ffn:
                        pre(0)
                    if pr is not None:
                        pair(i, pr)
                    if ffn:
                        pre(1)
                        act.wait_ge(hb_ready, kk * MH + MH + INIT)
                        act.wait_ge(th1_ready, kk + INIT)
                        nc.scalar.activation(th[:, :], hb[slot][:, :], ACT.Tanh, scale=0.5).then_inc(th_ready, 1)
                    if pr is not None:
                        pair(i, pr + 1)
                    if ffn:
                        act.wait_ge(th_ready, kk + 1)
                        nc.scalar.activation(th1[slot][:, :], th[:, :], ACT.Identity, bias=col(ONE)
                                             ).then_inc(th1_ready, 1)

                if ffn:
                    act.wait_ge(h2T_ps, s)
                    nc.scalar.copy(h2T[:, :], HBk[:, :]).then_inc(h2T_ready, 1)
                    act.wait_ge(lgd_ready, s)
                    nc.scalar.activation(ex[:, :], rp[:, :], ACT.Exp).then_inc(ex_ready, 1)
                    act.wait_ge(gT_ps, s)
                    nc.scalar.copy(gT[:, :], HA[0:E, :]).then_inc(gT_ready, 1)
                    expert(q * NE, 0, 0, None)
                    expert(q * NE + 1, 1, 0, None)
                with act.Fori(0, BODIES) as i:
                    for j in range(PER):
                        expert(q * NE + i * PER + (j + SHARED), j % 2, i, 2 * j if scan else None)
                if ffn:
                    act.wait_ge(yacc_ps, s)
                    nc.scalar.activation(yT[:, :], YACC[:, :], ACT.Identity, bias=col(BS2)).then_inc(yT_ready, 1)

            stage(0, True, False)
            with act.Fori(1, NC) as s:
                stage(s, True, True)
            stage(NC, False, True)

        @block.vector
        def _(dve):
            for started in (du_ready, s_done, p_done, q_done, m0_ready):
                dve.sem_inc(started, INIT)
            own = Chain(dve, dve_own)
            V = nc.vector
            dve.wait_ge(ld_w, 48)
            own(V.tensor_copy(sel_bf[:, :], cst("sel")[0:ROWS, :]))
            own(V.memset(S[SR - 1][:, :], 0.0))
            own(V.tensor_scalar(arep[:, :], cst("arep"), -5.0, 2.0, ALU.max, ALU.min))
            own(V.tensor_scalar(b2_sb[:, :], b2_sb[:, :], 2.0, None, ALU.mult))
            own.wait()
            nc.vector.engine_nop().then_inc(const_ready, 1)
            dve.wait_ge(mod_ps, 1)
            own(V.tensor_copy(mods[:, 0:3 * D], HA[:, 0:3 * D]))
            own(V.tensor_copy(mods[:, 3 * D:6 * D], HBk[:, 0:3 * D]))
            own.wait()
            for m in (CA, CB):
                own(V.tensor_scalar(m, m, 1.0, None, ALU.add))
            for i, g in enumerate((GA, GB)):
                own(V.scalar_tensor_tensor(out=gmag[:, i * D:(i + 1) * D], in0=g, scalar=-1.0, in1=g,
                                           op0=ALU.mult, op1=ALU.max))
                own(V.tensor_scalar(gsgn[:, i * D:(i + 1) * D], g, 0.0, 2.0, ALU.is_ge, ALU.mult))
            own.wait()
            own(V.tensor_scalar(gmag[:, :], gmag[:, :], 0.25, None, ALU.max))
            own.wait()
            for i, g in enumerate((GA, GB)):
                own(V.scalar_tensor_tensor(out=g, in0=gsgn[:, i * D:(i + 1) * D], scalar=-1.0,
                                           in1=gmag[:, i * D:(i + 1) * D], op0=ALU.add, op1=ALU.mult))
            own.wait()
            own(V.tensor_tensor(gg[:, :], GA, cst("lng"), ALU.mult))
            own(V.tensor_tensor(gbias[:, :], GA, cst("lnb"), ALU.mult))
            own.wait()
            V.engine_nop().then_inc(mod_ready, 1)

            def normalise(dst, src, n):
                for j in range(CT):
                    own(V.bn_stats(st[:, 6 * j:6 * j + 6], src(j)))
                own.wait()
                s3 = st[:, :].rearrange("p (j k) -> p j k", k=6)
                own(V.tensor_tensor(mean[:, :], s3[:, :, 1], s3[:, :, 4], ALU.add))
                own(V.tensor_tensor(mdif[:, :], s3[:, :, 1], s3[:, :, 4], ALU.subtract))
                own(V.tensor_tensor(vsum[:, :], s3[:, :, 2], s3[:, :, 5], ALU.add))
                own.wait()
                own(V.tensor_scalar(mean[:, :], mean[:, :], 0.5, None, ALU.mult))
                own(V.tensor_tensor(mdif[:, :], mdif[:, :], mdif[:, :], ALU.mult))
                own(V.tensor_scalar(vsum[:, :], vsum[:, :], 1.0 / D, EPS, ALU.mult, ALU.add))
                own.wait()
                V.scalar_tensor_tensor(out=vareps[:, :], in0=mdif[:, :], scalar=0.25, in1=vsum[:, :],
                                       op0=ALU.mult, op1=ALU.add).then_inc(var_ready, 1)
                dve.wait_ge(rstd_ready, n + 1)
                for j in range(CT):
                    own(V.tensor_scalar(dst[:, j * D:(j + 1) * D], src(j), mean[:, j:j + 1],
                                        rstd[:, j:j + 1], ALU.subtract, ALU.mult))
                own.wait()

            def by_feature(dst, a, b, op):
                return V.tensor_tensor(tiles(dst), tiles(a), over_tiles(b), op)

            dve.wait_ge(ld_x, 16)
            start, per = own.n, 2 * (2 * CT + 7)
            with dve.Fori(0, NC // 2) as c2:
                own.at(c2 * per + start)
                for u in range(2):
                    c = c2 * 2 + u
                    dve.wait_ge(hT_ps, c + INIT)
                    dve.wait_ge(hr_done, c + INIT)
                    normalise(Hn[u], lambda j: X[:, bass.ds(c * CW + j * D, D)], c)
                    own(by_feature(Hn[u][:, :], Hn[u][:, :], CA, ALU.mult))
                    own.wait()
                    by_feature(Hn[u][:, :], Hn[u][:, :], SA, ALU.add).then_inc(h_ready, 1)
                assert own.n == per
            own.at(start + NC // 2 * per)

            dve.wait_ge(xc_ready, NC)
            half = T * B // 2
            for h in range(2):
                def tap(k):
                    return XC[:, h * half + k * B:h * half + k * B + half]

                y = XS[:, h * half:(h + 1) * half]
                own(V.tensor_scalar(y, tap(0), col(CONV_W), col(CONV_B), ALU.mult, ALU.add))
                for k in range(1, KW):
                    own.wait()
                    ins = V.scalar_tensor_tensor(out=y, in0=tap(k), scalar=col(CONV_W + k), in1=y,
                                                 op0=ALU.mult, op1=ALU.add)
                    if k < KW - 1:
                        own(ins)
                ins.then_inc(conv_done, 1)

            with dve.Fori(0, NC // 2) as c2:
                for u in range(2):
                    c = c2 * 2 + u
                    dve.wait_ge(dt_ps, c + 1)
                    dve.wait_ge(dte_ready, c + INIT)
                    by_feature(dti[:, :], U0[:, :], cst("dtb"), ALU.add).then_inc(dti_ready, 1)
                    dve.wait_ge(dtl_ready, c + 1)
                    dve.wait_ge(part_ready[u], c2 * PARTS + INIT)
                    V.tensor_scalar(DU[u][:, 0:CW], dtl[:, :], 0.001, 0.2, ALU.max, ALU.min
                                    ).then_inc(dt_clipped, 1)
                    dve.wait_ge(dt_clipped, c + 1)
                    V.tensor_tensor(DU[u][:, CW:2 * CW], DU[u][:, 0:CW], U1[:, :], ALU.mult
                                    ).then_inc(du_ready, 1)
            dve.wait_ge(aexp_ready, 1)
            V.tensor_scalar(arep[:, :], arep[:, :], -1.0, None, ALU.mult).then_inc(arep_ready, 1)
            dve.wait_ge(bcol_ready, 1)
            b3 = BCOL[:, :].rearrange("p (h t) -> p h t", h=2)
            own(V.memset(b3[:, :, T:T + GT], 0.0))

            def group_scalars(g, slot):
                V.tensor_copy(BNOW[slot][:, :].rearrange("p (h t) -> p h t", h=2),
                              b3[:, :, bass.ds(g * GT, GT)]).then_inc(b_ready, 1)

            own.wait()
            group_scalars(0, 0)
            before = own.base + own.n
            per_stage = 4 * CT + 33

            def stage(s, scan, ffn):
                q = s - 1

                def step(i, n, h):
                    p = s * (TC // 2) + i * PAIRS + n
                    t = s * TC + i * (2 * PAIRS) + (2 * n + h)
                    now, prev = S[(2 * n + h) % SR], S[(2 * n + h - 1) % SR]
                    if h == 0:
                        dve.wait_ge(a_ready, p + 1)
                        dve.wait_ge(u_bc, p + 1)
                        dve.wait_ge(y_done, t + 2)
                        if n % 4 == 0:
                            dve.wait_ge(b_ready, s * (TC // GT) + i * 2 + (n // 4 + 1))
                    dve.wait_ge(s_done, t + INIT)
                    V.tensor_tensor(pt[:, :], prev[:, :], ab[n % 2][:, h * SW:(h + 1) * SW], ALU.mult
                                    ).then_inc(p_done, 1)
                    if n % 4 == 2 and h == 0:
                        group_scalars(s * (TC // GT) + i * 2 + (n // 4 + 1), 1 - n // 4)
                    dve.wait_ge(p_done, t + 1 + INIT)
                    for half in range(2):
                        k = half * GT + 2 * n % GT + h
                        r = slice(half * D, (half + 1) * D)
                        V.scalar_tensor_tensor(out=qt[:, r], in0=U[n % 2][:, h * SW + half * D:h * SW + (half + 1) * D],
                                               scalar=BNOW[n // 4][:, k:k + 1], in1=pt[:, r],
                                               op0=ALU.mult, op1=ALU.add).then_inc(q_done, 1)
                    dve.wait_ge(q_done, t * 2 + 2 + INIT)
                    V.tensor_scalar(now[:, :], qt[:, :], 10.0, -10.0, ALU.min, ALU.max).then_inc(s_done, 1)

                def gate(kk, slot, m):
                    dve.wait_ge(hb_ready, kk * MH + (m + 1) + INIT)
                    dve.wait_ge(h11_ps, kk * MH + (m + 1))
                    r = slice(m * CW, (m + 1) * CW)
                    V.scalar_tensor_tensor(out=m0[slot][:, r], in0=(HBk, HC)[m][:, :],
                                           scalar=W1S[slot][:, 2 * H + MH + m:2 * H + MH + m + 1],
                                           in1=hb[slot][:, r], op0=ALU.add, op1=ALU.mult).then_inc(m0_ready, 1)

                if ffn:
                    own.at(q * per_stage + before)
                    cols = bass.ds(q * CW, CW)
                    dve.wait_ge(y_done, s * TC + SR)
                    V.tensor_tensor(ygT[:, :], YSC[:, :], ZG[:, cols], ALU.mult).then_inc(yg_ready, 1)
                    dve.wait_ge(o_ps, s)
                    own(V.tensor_tensor(om[:, :], HA[:, :], HR[:, cols], ALU.add))
                    own.wait()
                    normalise(om, lambda j: om[:, j * D:(j + 1) * D], q * 2 + NC)
                    own(by_feature(om[:, :], om[:, :], gg[:, :], ALU.mult))
                    own.wait()
                    own(V.tensor_tensor(X2[:, :], om[:, :], X[:, cols], ALU.add))
                    own.wait()
                    normalise(Hn[0], lambda j: X2[:, j * D:(j + 1) * D], q * 2 + (NC + 1))
                    own(by_feature(Hn[0][:, :], Hn[0][:, :], CB, ALU.mult))
                    own.wait()
                    by_feature(Hn[0][:, :], Hn[0][:, :], SB, ALU.add).then_inc(h2_ready, 1)

                    def e3(ap):
                        return ap.rearrange("p (j e) -> p j e", e=E)

                    def over_e(ap):
                        return ap.unsqueeze(2).broadcast_to([P, CT, E])

                    order = cst("order").unsqueeze(1).broadcast_to([P, CT, E])
                    dve.wait_ge(lg_ps, s)
                    own(V.tensor_copy(lg[:, :], HC[:, 0:CT * E]))
                    own.wait()

                    def first_largest(top, src, pick):
                        own(V.tensor_reduce(top, e3(src), AX.X, ALU.max))
                        own.wait()
                        own(V.tensor_tensor(e3(pick), e3(src), over_e(top), ALU.is_equal))
                        own.wait()
                        own(V.tensor_tensor(e3(pick), e3(pick), order, ALU.mult))
                        own.wait()
                        own(V.tensor_reduce(place[:, :], e3(pick), AX.X, ALU.max))
                        own.wait()
                        own(V.tensor_tensor(e3(pick), e3(pick), over_e(place[:, :]), ALU.is_equal))
                        own.wait()

                    first_largest(top[:, :], lg[:, :], pick1[:, :])
                    V.tensor_tensor(e3(rp[:, :]), e3(lg[:, :]), over_e(top[:, :]), ALU.subtract
                                    ).then_inc(lgd_ready, 1)
                    own(V.scalar_tensor_tensor(out=lg[:, :], in0=pick1[:, :], scalar=-1e38, in1=lg[:, :],
                                               op0=ALU.mult, op1=ALU.add))
                    own.wait()
                    first_largest(top2[:, :], lg[:, :], pick2[:, :])
                    own(V.tensor_tensor(pick1[:, :], pick1[:, :], pick2[:, :], ALU.add))
                    own.wait()
                    dve.wait_ge(ex_ready, s)
                    own(V.tensor_tensor(ex[:, :], ex[:, :], pick1[:, :], ALU.mult))
                    own.wait()
                    own(V.tensor_reduce(gsum[:, :], e3(ex[:, :]), AX.X, ALU.add))
                    own.wait()
                    own(V.reciprocal(grec[:, :], gsum[:, :]))
                    own.wait()
                    V.scalar_tensor_tensor(out=e3(gt[:, :]), in0=e3(ex[:, :]), scalar=0.5, in1=over_e(grec[:, :]),
                                           op0=ALU.mult, op1=ALU.mult).then_inc(gt_ready, 1)
                    for k in range(SHARED):
                        for m in range(MH):
                            gate(q * NE + k, k, m)
                with dve.Fori(0, BODIES) as i:
                    for j in range(PER):
                        kk = q * NE + i * PER + (j + SHARED)
                        if scan:
                            step(i, 2 * j, 0)
                            step(i, 2 * j, 1)
                        if ffn:
                            gate(kk, j % 2, 0)
                        if scan:
                            step(i, 2 * j + 1, 0)
                        if ffn:
                            gate(kk, j % 2, 1)
                        if scan:
                            step(i, 2 * j + 1, 1)
                if ffn:
                    dve.wait_ge(yt_ps, s)
                    dve.wait_ge(stored, q * 16 + 16 * INIT)
                    own(by_feature(O[:, :], HBk[:, :], GB, ALU.mult))
                    own.wait()
                    V.tensor_tensor(O[:, :], O[:, :], X2[:, :], ALU.add).then_inc(out_ready, 1)
                    assert own.n == per_stage, own.n

            stage(0, True, False)
            with dve.Fori(1, NC) as s:
                stage(s, True, True)
            stage(NC, False, True)


def kernel(**inputs):
    import numpy as np
    import concourse.bacc as bacc
    from concourse.bass_utils import run_bass_kernel_spmd

    g = {k: np.asarray(v) for k, v in inputs.items()}

    def a(name):
        return g["L0_attn_" + name]

    def f(name):
        return g["L0_ffn_" + name]

    def row(v):
        return np.broadcast_to(v[None, :], (P, v.shape[0]))

    def hidden_cols(v):
        return v.reshape(MH, P).T

    d = D
    sel = np.zeros((P, P), np.float32)
    for r in range(ROWS):
        sel[r, N * (r % HB):N * (r % HB) + N] = 1.0
    cols = np.zeros((P, 16), np.float32)
    cols[:, 0:2] = a("in_proj_b").reshape(2, d).T
    cols[:, 2:6] = a("conv_w")[:, 0, :]
    cols[:, 6] = a("conv_b")
    cols[:, 7] = np.tile(a("B_b"), HB)
    cols[:, 8] = np.tile(a("C_b"), HB)
    cols[:, 9] = f("bs2")
    cols[:, 10] = 1.0
    wcol = np.concatenate([
        a("in_proj_w").T, a("dt_w").T, a("B_w").T, a("C_w").T, a("out_w").T, f("Wg"),
        np.tile(a("A_log").T, (HB, 1)), np.eye(P, dtype=np.float32), np.tile(g["L0_c"].T, (1, TT)), cols,
        row(a("dt_b")), row(a("out_b")), row(a("ln_g")), row(a("ln_beta")), sel,
        row(np.arange(E, 0, -1).astype(np.float32)),
    ], axis=1)
    w1s = [np.concatenate([f("Ws1")[:, k * H:(k + 1) * H], f("Ws11")[:, k * H:(k + 1) * H],
                           hidden_cols(f("bs1")[k * H:(k + 1) * H]), hidden_cols(f("bs11")[k * H:(k + 1) * H])], axis=1)
           for k in range(SHARED)]
    w1r = [np.concatenate([f("W1")[e], f("W11")[e], hidden_cols(f("b1")[e]), hidden_cols(f("b11")[e])], axis=1)
           for e in range(E)]

    def second(w):
        return w.reshape(MH, P, D).transpose(1, 0, 2).reshape(P, MH * D)

    w2s = [second(f("Ws2")[k * H:(k + 1) * H]) for k in range(SHARED)] + [second(f("W2")[e]) for e in range(E)]
    nt = T // TT
    xt = a("x").reshape(B, nt, TT, D).transpose(2, 0, 1, 3).reshape(P, nt * D)
    arrays = {
        "in_x": xt, "in_wcol": wcol, "in_wmod": g["L0_wmod"], "in_w1": np.stack(w1s + w1r),
        "in_w2": np.stack(w2s), "in_b2": f("b2"),
    }
    arrays = {k: np.ascontiguousarray(v) for k, v in arrays.items()}
    nc = bacc.Bacc("TRN2", target_bir_lowering=False, num_devices=1)
    aps = {k: nc.dram_tensor(k, v.shape, mybir.dt.from_np(v.dtype), kind="ExternalInput").ap()
           for k, v in arrays.items()}
    out = nc.dram_tensor("out_0", (P, nt * D), F32, kind="ExternalOutput").ap()
    build(nc, aps["in_x"], aps["in_wcol"], aps["in_wmod"], aps["in_w1"], aps["in_w2"], aps["in_b2"], out)
    r = run_bass_kernel_spmd(nc, [arrays], core_ids=[0])
    y = r.results[0]["out_0"]
    return y.reshape(TT, B, nt, D).transpose(1, 2, 0, 3).reshape(B, T, D)
```

```python
from contextlib import ExitStack

import concourse.bass as bass
from concourse import mybir

F32 = mybir.dt.float32
BF16 = mybir.dt.bfloat16
ALU = mybir.AluOpType
ACT = mybir.ActivationFunctionType
AX = mybir.AxisListType

B, T, D, N = 8, 512, 128, 32
E, H, HS = 16, 256, 512
P = 128
TT = P // B
TC = 64
NC = T // TC
CT = TC // TT
CW = TC * B
HB = B // 2
GT = 8
NG = T // GT
PARTS = 3
ROWS = PARTS * HB
SW = 2 * D
GW = 2 * GT * SW
SHARED = HS // H
NE = SHARED + E
MH = H // P
PER = 4
PAIRS = 2 * PER
BODIES = E // PER
EPS = 1e-5
XPAD = 2
KW = 4
INIT = 2
STORES = CT * PARTS * TT // GT


class Chain:

    def __init__(self, eng, sem):
        self.eng, self.sem, self.base, self.n = eng, sem, 0, 0

    def at(self, base):
        self.base, self.n = base, 0

    def __call__(self, ins):
        ins.then_inc(self.sem, 1)
        self.n += 1

    def wait(self):
        self.eng.wait_ge(self.sem, self.base + self.n)


def build(nc, x, wcol, wmod, w1, w2, b2, out):
    with ExitStack() as ctx:
        def sb(name, cols, dt=F32, parts=P):
            return ctx.enter_context(nc.sbuf_tensor(name, [parts, cols], dt))

        def bank(name):
            return ctx.enter_context(nc.psum_tensor(name, [P, 512], F32))

        def sem(name):
            return ctx.enter_context(nc.semaphore(name))

        names = dict(win=2 * D, wdt=D, wb=N, wc=N, wout=D, wg=E, arep=D, ident=D, ct=P, cols=16,
                     dtb=D, outb=D, lng=D, lnb=D, sel=P, order=E)
        at, o = {}, 0
        for k, v in names.items():
            at[k] = (o, o + v)
            o += v
        wc_sb = sb("wc_sb", o)

        def cst(name):
            a, b = at[name]
            return wc_sb[:, a:b]

        c0 = at["cols"][0]

        def col(i):
            return wc_sb[:, c0 + i:c0 + i + 1]

        IN_B, CONV_W, CONV_B, B_B, C_B, BS2, ONE = 0, 2, 6, 7, 8, 9, 10
        wmod_sb = sb("wmod_sb", 6 * D)
        sct = sb("sct", P)
        sel_bf = sb("sel_bf", P, BF16, ROWS)
        b2_sb = sb("b2_sb", D, F32, E)
        mods = sb("mods", 6 * D)
        SA, CA, GA, SB, CB, GB = (mods[:, i * D:(i + 1) * D] for i in range(6))
        gmag = sb("gmag", 2 * D)
        gsgn = sb("gsgn", 2 * D)
        arep = sb("arep", D)
        gg = sb("gg", D)
        gbias = sb("gbias", D)
        mexp = sb("mexp", CT)
        half_gate = sb("half_gate", CW)

        X = sb("X", T * B * D // P)
        HR = sb("HR", T * B * D // P)
        ZG = sb("ZG", T * B)
        XC = sb("XC", (T + KW - 1) * B)
        XS = sb("XS", T * B)
        BCOL = sb("BCOL", 2 * (T + GT))
        BNOW = [sb(f"BNOW{i}", 2 * GT) for i in range(2)]
        CBLK = sb("CBLK", T * B)

        st = sb("st", CT * 6)
        mean, mdif, vsum = (sb(n, CT) for n in ("mean", "mdif", "vsum"))
        vareps = sb("vareps", CT)
        rstd = sb("rstd", CT)
        Hn = [sb(f"Hn{i}", CW) for i in range(2)]
        hT = [sb(f"hT{i}", CW) for i in range(2)]
        dti = sb("dti", CW)
        dte = sb("dte", CW)
        dtl = sb("dtl", CW)
        DU = [sb(f"DU{i}", 2 * CW) for i in range(2)]
        res1 = sb("res1", 2 * CW)
        res2 = sb("res2", 2 * CW)
        PB = [sb(f"PB{i}", PARTS * 2 * CW, BF16) for i in range(2)]
        R = [sb(f"R{i}", GW, BF16, ROWS) for i in range(2)]
        dtc = [sb(f"dtc{i}", 2 * SW) for i in range(2)]
        dta = [sb(f"dta{i}", 2 * SW) for i in range(2)]
        ab = [sb(f"ab{i}", 2 * SW) for i in range(2)]
        SR = 8
        S = [sb(f"S{i}", SW) for i in range(SR)]
        pt = sb("pt", SW)
        qt = sb("qt", SW)
        W1S = [sb(f"W1S{i}", 2 * H + 2 * MH) for i in range(2)]
        W2S = [sb(f"W2S{i}", MH * D) for i in range(2)]
        GS = [dti, dte]
        hid = [t[:, i * MH * CW:(i + 1) * MH * CW] for t in (XS, XC) for i in range(4)]
        hb, th1, m0, th, wg_ = hid[0:2], hid[2:4], hid[4:6], hid[6], hid[7]
        hh = DU
        ygT = hT[0]
        om, X2, O = hT[0], res1[:, CW:2 * CW], res2[:, 0:CW]
        h2T = hT[1]
        lg = sb("lg", CT * E)
        top, top2, place = (sb(n, CT) for n in ("top", "top2", "place"))
        pick1, pick2 = (sb(n, CT * E) for n in ("pick1", "pick2"))
        rp = sb("rp", CT * E)
        ex = sb("ex", CT * E)
        gsum = sb("gsum", CT)
        grec = sb("grec", CT)
        gt = sb("gt", CT * E)
        gT, yT = dtl[0:E, :], res2[:, CW:2 * CW]

        YACC, YSC, DTB, U0, U1, HA, HBk, HC = (
            bank(n) for n in ("YACC", "YSC", "DTB", "U0", "U1", "HA", "HBk", "HC"))
        U = [U0, U1]

        DS = nc.dram_tensor("scan_rows", ((NG + 2) * ROWS, GW), BF16).ap()
        GD = nc.dram_tensor("gate_rows", (NE, CW), F32).ap()

        ld_x, ld_w = sem("ld_x"), sem("ld_w")
        dve_own = sem("dve_own")
        pool_const = sem("pool_const")
        sct_ready, mod_ps, mod_ready = sem("sct_ready"), sem("mod_ps"), sem("mod_ready")
        var_ready, rstd_ready = sem("var_ready"), sem("rstd_ready")
        h_ready, hr_done, xg_done = sem("h_ready"), sem("hr_done"), sem("xg_done")
        hT_ps, hT_ready, inp_ps, xc_ready, z_ready = (
            sem(n) for n in ("hT_ps", "hT_ready", "inp_ps", "xc_ready", "z_ready"))
        conv_done, xs_ready, bc_ps, bcol_ready = (
            sem(n) for n in ("conv_done", "xs_ready", "bc_ps", "bcol_ready"))
        xst_ready, dt_ps, dti_ready, dte_ready, dtl_ready, du_ready = (
            sem(n) for n in ("xst_ready", "dt_ps", "dti_ready", "dte_ready", "dtl_ready", "du_ready"))
        part_ready = [sem(f"part_ready{i}") for i in range(2)]
        ds_stored = [sem(f"ds_stored{i}") for i in range(2)]
        res_ready = sem("res_ready")
        r_loaded = [sem(f"r_loaded{i}") for i in range(2)]
        dt_bc, u_bc, dtc_ready, dta_ready, a_ready = (
            sem(n) for n in ("dt_bc", "u_bc", "dtc_ready", "dta_ready", "a_ready"))
        b_ready = sem("b_ready")
        p_done, q_done, s_done, y_done = (sem(n) for n in ("p_done", "q_done", "s_done", "y_done"))
        w1_loaded = [sem(f"w1_loaded{i}") for i in range(2)]
        w2_loaded = [sem(f"w2_loaded{i}") for i in range(2)]
        g_loaded = [sem(f"g_loaded{i}") for i in range(2)]
        h1_ps, h11_ps, hb_ready, th_ready, th1_ready = (
            sem(n) for n in ("h1_ps", "h11_ps", "hb_ready", "th_ready", "th1_ready"))
        m0_ready, wg_ready, hh_ready, w2_done = (
            sem(n) for n in ("m0_ready", "wg_ready", "hh_ready", "w2_done"))
        yg_ready, o_ps, h2_ready, h2T_ps, h2T_ready, lg_ps = (
            sem(n) for n in ("yg_ready", "o_ps", "h2_ready", "h2T_ps", "h2T_ready", "lg_ps"))
        lgd_ready, ex_ready, gt_ready, gT_ps, gT_ready, gd_stored = (
            sem(n) for n in ("lgd_ready", "ex_ready", "gt_ready", "gT_ps", "gT_ready", "gd_stored"))
        const_ready, aexp_ready, arep_ready = sem("const_ready"), sem("aexp_ready"), sem("arep_ready")
        zero_rows, dt_clipped = sem("zero_rows"), sem("dt_clipped")
        yT_ready, yt_ps, out_ready, stored = (
            sem(n) for n in ("yT_ready", "yt_ps", "out_ready", "stored"))

        def tiles(ap, w=D):
            return ap.rearrange("p (j d) -> p j d", d=w)

        def over_tiles(ap, n=CT):
            return ap.unsqueeze(1).broadcast_to([P, n, D])

        block = ctx.enter_context(nc.Block())

        @block.sync
        def _(sp):
            for x_stored in (*ds_stored, stored):
                sp.sem_inc(x_stored, 16 * INIT)
            sp.dma_start(wc_sb[:, :], wcol).then_inc(ld_w, 16)
            sp.dma_start(wmod_sb[:, :], wmod).then_inc(ld_w, 16)
            sp.dma_start(b2_sb[:, :], b2).then_inc(ld_w, 16)
            sp.dma_start(X[:, :], x).then_inc(ld_x, 16)

            sp.wait_ge(pool_const, 3)
            zeros = S[0][0:ROWS, :].bitcast(BF16)
            for g in range(NG, NG + 2):
                for c in range(8):
                    sp.dma_start(DS[g * ROWS:(g + 1) * ROWS, c * GW // 8:(c + 1) * GW // 8], zeros
                                 ).then_inc(zero_rows, 16)
            dv = DS.rearrange("(g m b) (q t h d) -> g m t h b q d", m=PARTS, b=HB, q=2, h=2, d=D)
            with sp.Fori(0, NC // 2) as c2:
                for u in range(2):
                    sp.wait_ge(part_ready[u], (c2 + 1) * PARTS + INIT)
                    src = PB[u][:, :].rearrange("p (m q j d) -> p m q j d", m=PARTS, q=2, d=D)
                    for j in range(CT):
                        for m in range(PARTS):
                            for tg in range(TT // GT):
                                g = c2 * (2 * CT * TT // GT) + (u * CT + j) * (TT // GT) + tg
                                sp.dma_start(
                                    dv[bass.ds(g, 1), m].rearrange("g t h b q d -> (g t h) b q d"),
                                    src[64 * tg:64 * tg + 64, m, :, j, :]).then_inc(ds_stored[u], 16)
            sp.wait_ge(zero_rows, 16 * 16)
            for u in range(2):
                sp.wait_ge(ds_stored[u], STORES * (NC // 2) * 16 + 16 * INIT)

            def load_rows(g, slot):
                sp.dma_start(R[slot][:, :], DS[bass.ds(g * ROWS, ROWS), :]).then_inc(r_loaded[slot], 16)

            def load_expert(dst, src, k, loaded):
                sp.dma_start(dst[:, :], src[bass.ds(k, 1)].rearrange("a p f -> (a p) f")).then_inc(loaded, 16)

            def load_gate(k, slot):
                sp.dma_start(GS[slot][:, :], GD[bass.ds(k, 1), :].broadcast_to([P, CW])
                             ).then_inc(g_loaded[slot], 16)

            load_rows(0, 0)
            load_rows(1, 1)
            sp.wait_ge(pool_const, 5)
            sp.dma_start(GD[0:SHARED, :], half_gate[0:SHARED, :]).then_inc(gd_stored, 16)

            def stage(s, scan, ffn):
                q = s - 1
                with sp.Fori(0, BODIES) as i:
                    for j in range(PER):
                        if ffn:
                            k = i * PER + j + SHARED
                            kk = q * NE + k
                            slot = j % 2
                            sp.wait_ge(m0_ready, (kk - 1) * MH + INIT)
                            load_expert(W1S[slot], w1, k, w1_loaded[slot])
                            sp.wait_ge(wg_ready, kk - 1 + INIT)
                            sp.wait_ge(gd_stored, s * 16 + 16)
                            load_gate(k, slot)
                            sp.wait_ge(w2_done, kk - 2 + INIT)
                            load_expert(W2S[1 - slot], w2, k - 1, w2_loaded[1 - slot])
                        if scan and j % 2:
                            g = s * (TC // GT) + i * 2 + j // 2
                            sp.wait_ge(u_bc, g * (GT // 2) + GT // 2)
                            sp.wait_ge(dt_bc, g * (GT // 2) + GT // 2)
                            load_rows(g + 2, j // 2)
                if ffn:
                    sp.wait_ge(w2_done, s * NE - 2 + INIT)
                    load_expert(W2S[1], w2, NE - 1, w2_loaded[1])
                if scan:
                    for k in range(SHARED):
                        if ffn:
                            sp.wait_ge(m0_ready, (s * NE + (k - 1)) * MH + INIT)
                        load_expert(W1S[k], w1, k, w1_loaded[k])
                    for k in range(SHARED):
                        if ffn:
                            sp.wait_ge(wg_ready, s * NE + (k - 1) + INIT)
                        else:
                            sp.wait_ge(gd_stored, 16)
                        load_gate(k, k)
                    if ffn:
                        sp.wait_ge(w2_done, s * NE - 1 + INIT)
                    load_expert(W2S[0], w2, 0, w2_loaded[0])
                if ffn:
                    sp.wait_ge(out_ready, s)
                    sp.dma_start(out[:, bass.ds(q * CW, CW)], O[:, :]).then_inc(stored, 16)
                if scan:
                    sp.wait_ge(gT_ready, s + 1)
                    sp.dma_start(GD[SHARED:NE, :], gT[:, :]).then_inc(gd_stored, 16)

            stage(0, True, False)
            with sp.Fori(1, NC) as s:
                stage(s, True, True)
            stage(NC, False, True)
            sp.wait_ge(stored, 16 * NC + 16 * INIT)
            for r in r_loaded:
                sp.wait_ge(r, (1 + NC * BODIES) * 16)

        @block.gpsimd
        def _(pool):
            for started in (hr_done, hh_ready, wg_ready):
                pool.sem_inc(started, INIT)
            nc.gpsimd.memset(S[0][:, :], 0.0).then_inc(pool_const, 1)
            nc.gpsimd.memset(CBLK[:, :], 0.0).then_inc(pool_const, 1)
            nc.gpsimd.memset(XC[:, :], 0.0).then_inc(pool_const, 1)
            nc.gpsimd.memset(mexp[:, :], -0.5).then_inc(pool_const, 1)
            nc.gpsimd.memset(half_gate[:, :], 0.5).then_inc(pool_const, 1)
            pool.wait_ge(pool_const, 5)

            def inv_std(n):
                pool.wait_ge(var_ready, n + 1)
                nc.gpsimd.tensor_tensor(rstd[:, :], vareps[:, :], mexp[:, :], ALU.pow).then_inc(rstd_ready, 1)

            with pool.Fori(0, NC // 2) as c2:
                for u in range(2):
                    c = c2 * 2 + u
                    inv_std(c)
                    pool.wait_ge(h_ready, c + 1)
                    cols = bass.ds(c2 * (2 * CW) + u * CW, CW)
                    nc.gpsimd.tensor_tensor(tiles(HR[:, cols]), tiles(Hn[u][:, :]), over_tiles(cst("outb")),
                                            ALU.add).then_inc(hr_done, 1)
                    nc.gpsimd.tensor_tensor(tiles(X[:, cols]), tiles(X[:, cols]), over_tiles(gbias[:, :]),
                                            ALU.add).then_inc(xg_done, 1)

            with pool.Fori(0, NC // 2) as c2:
                for u in range(2):
                    c = c2 * 2 + u
                    part = PB[u][:, :].rearrange("p (m f) -> p m f", m=PARTS)
                    pool.wait_ge(part_ready[u], c2 * PARTS + 1 + INIT)
                    nc.gpsimd.tensor_tensor(res1[:, :], DU[u][:, :], part[:, 0, :], ALU.subtract
                                            ).then_inc(res_ready, 1)
                    pool.wait_ge(part_ready[u], c2 * PARTS + 2 + INIT)
                    pool.wait_ge(res_ready, c * 2 + 1)
                    nc.gpsimd.tensor_tensor(res2[:, :], res1[:, :], part[:, 1, :], ALU.subtract
                                            ).then_inc(res_ready, 1)

            def dt_times_a(p, slot):
                pool.wait_ge(dtc_ready, p + 1)
                nc.gpsimd.tensor_tensor(tiles(dta[slot][:, :]), tiles(dtc[slot][:, :]), over_tiles(arep[:, :]),
                                        ALU.mult).then_inc(dta_ready, 1)

            def gated(kk, slot):
                pool.wait_ge(th1_ready, kk + 1 + INIT)
                pool.wait_ge(hh_ready, kk + INIT)
                nc.gpsimd.tensor_tensor(wg_[:, :].rearrange("p (m f) -> p m f", m=MH),
                                        th1[slot][:, :].rearrange("p (m f) -> p m f", m=MH),
                                        GS[slot][:, :].unsqueeze(1).broadcast_to([P, MH, CW]), ALU.mult
                                        ).then_inc(wg_ready, 1)

            def hidden(kk, slot):
                pool.wait_ge(m0_ready, (kk + 1) * MH + INIT)
                pool.wait_ge(wg_ready, kk + 1 + INIT)
                pool.wait_ge(w2_done, kk - 1 + INIT)
                nc.gpsimd.tensor_tensor(hh[slot][:, :], m0[slot][:, :], wg_[:, :], ALU.mult
                                        ).then_inc(hh_ready, 1)

            pool.wait_ge(arep_ready, 1)
            dt_times_a(0, 0)
            dt_times_a(1, 1)

            def stage(s, scan, ffn):
                q = s - 1

                def expert(kk, n, slot, prev, p):
                    if prev:
                        pool.wait_ge(g_loaded[1 - slot], n * 16)
                        gated(kk - 1, 1 - slot)
                    if p is not None:
                        pool.wait_ge(a_ready, p + 1)
                        dt_times_a(p + 2, 0)
                    if prev:
                        hidden(kk - 1, 1 - slot)
                    if p is not None:
                        pool.wait_ge(a_ready, p + 2)
                        dt_times_a(p + 3, 1)

                with pool.Fori(0, BODIES) as i:
                    for j in range(PER):
                        p = s * (TC // 2) + i * PAIRS + 2 * j
                        kk = q * NE + i * PER + (j + SHARED)
                        n = q * (NE // 2) + i * 2 + (1 + (j + 1) // 2)
                        expert(kk, n, j % 2, ffn, p if scan else None)
                if ffn:
                    expert(s * NE, s * (NE // 2), 0, True, None)
                if scan:
                    inv_std(s * 2 + NC)
                    inv_std(s * 2 + (NC + 1))
                    expert(s * NE + 1, s * (NE // 2) + 1, 1, True, None)

            stage(0, True, False)
            with pool.Fori(1, NC) as s:
                stage(s, True, True)
            stage(NC, False, True)

        @block.tensor
        def _(pe):
            for started in (hT_ps, w2_done):
                pe.sem_inc(started, INIT)
            pe.sem_inc(y_done, SR)
            pe.wait_ge(ld_w, 48)
            pe.wait_ge(sct_ready, 1)
            nc.tensor.matmul(HA[:, 0:3 * D], sct[:, :], wmod_sb[:, 0:3 * D], start=True, stop=True)
            nc.tensor.matmul(HBk[:, 0:3 * D], sct[:, :], wmod_sb[:, 3 * D:6 * D], start=True, stop=True
                             ).then_inc(mod_ps, 1)
            pe.wait_ge(mod_ready, 1)
            ident = cst("ident")

            with pe.Fori(0, NC // 2) as c2:
                for u in range(2):
                    c = c2 * 2 + u
                    pe.wait_ge(h_ready, c + 1)
                    pe.wait_ge(hT_ready, c + INIT)
                    for j in range(CT):
                        mm = nc.tensor.transpose(HA[:, j * D:(j + 1) * D], Hn[u][:, j * D:(j + 1) * D], ident)
                    mm.then_inc(hT_ps, 1)
                    pe.wait_ge(hT_ready, c + 1 + INIT)
                    pe.wait_ge(z_ready, c + INIT)
                    nc.tensor.matmul(HBk[:, :], cst("win")[:, 0:D], hT[u][:, :], start=True, stop=True
                                     ).then_inc(inp_ps, 1)
                    nc.tensor.matmul(HC[:, :], cst("win")[:, D:2 * D], hT[u][:, :], start=True, stop=True
                                     ).then_inc(inp_ps, 1)

            pe.wait_ge(xs_ready, 2)
            xs3 = XS[:, :].rearrange("p (t b) -> p t b", b=B)
            for w, banks in (("wb", (HA, HBk)), ("wc", (HC, DTB))):
                for b in range(B):
                    mm = nc.tensor.matmul(banks[b // HB][N * (b % HB):N * (b % HB) + N, :], cst(w),
                                          xs3[:, :, b], start=True, stop=True)
            mm.then_inc(bc_ps, 1)

            with pe.Fori(0, NC // 2) as c2:
                for u in range(2):
                    c = c2 * 2 + u
                    pe.wait_ge(xst_ready, c + 1)
                    pe.wait_ge(du_ready, c + INIT)
                    for j in range(CT):
                        nc.tensor.matmul(U0[:, j * D:(j + 1) * D], hT[u][:, j * D:(j + 1) * D], cst("wdt"),
                                         start=True, stop=True)
                    for j in range(CT):
                        mm = nc.tensor.transpose(U1[:, j * D:(j + 1) * D], hT[u][:, j * D:(j + 1) * D], ident)
                    mm.then_inc(dt_ps, 1)

            def spread(bnk, n, what, ready):
                c = what * GW // 2 + n % 4 * 2 * SW
                nc.tensor.matmul(bnk[:, :], sel_bf[:, :], R[n // 4 % 2][:, c:c + 2 * SW], start=True, stop=True
                                 ).then_inc(ready, 1)

            pe.wait_ge(du_ready, NC + INIT)
            pe.wait_ge(bcol_ready, 1)
            pe.wait_ge(r_loaded[0], 16)
            spread(U[0], 0, 1, u_bc)
            spread(DTB, 0, 0, dt_bc)
            pe.wait_ge(dtc_ready, 1)
            spread(DTB, 1, 0, dt_bc)

            def stage(s, scan, ffn):
                q = s - 1

                def readout(i, n):
                    for h in range(2):
                        tl = i * (2 * PAIRS) + (2 * n + h)
                        pe.wait_ge(s_done, s * TC + tl + 1 + INIT)
                        for half in range(2):
                            mm = nc.tensor.matmul(
                                YSC[:, bass.ds(tl * B + half * HB, HB)],
                                S[(2 * n + h) % SR][:, half * D:(half + 1) * D],
                                CBLK[:, bass.ds((s * TC + tl) * B + half * HB, HB)], start=True, stop=True)
                        mm.then_inc(y_done, 1)

                def pair(i, n):
                    p = s * (TC // 2) + i * PAIRS + n
                    body = s * BODIES + i
                    if n:
                        readout(i, n - 1)
                    if (n + 1) % 4 == 0:
                        pe.wait_ge(r_loaded[(n + 1) // 4 % 2], (body + 1 + (n + 1) // 8) * 16)
                    pe.wait_ge(q_done, p * 4 + INIT)
                    spread(U[(n + 1) % 2], n + 1, 1, u_bc)
                    if (n + 2) % 4 == 0:
                        pe.wait_ge(r_loaded[(n + 2) // 4 % 2], (body + 1 + (n + 2) // 8) * 16)
                    pe.wait_ge(dtc_ready, p + 2)
                    spread(DTB, n + 2, 0, dt_bc)

                def second(kk, n, slot, m, last=False):
                    if m == 0:
                        pe.wait_ge(hh_ready, kk + 1 + INIT)
                        pe.wait_ge(w2_loaded[slot], n * 16)
                    mm = nc.tensor.matmul(YACC[:, :], W2S[slot][:, m * D:(m + 1) * D],
                                          hh[slot][:, m * CW:(m + 1) * CW],
                                          start=False, stop=last, skip_group_check=True)
                    if m == MH - 1:
                        mm.then_inc(w2_done, 1)

                def expert(kk, n, slot, prev, i, pr):
                    w = W1S[slot]
                    for m in range(MH):
                        if kk is not None:
                            if m == 0:
                                pe.wait_ge(w1_loaded[slot], n * 16)
                            pe.wait_ge(hb_ready, kk * MH + m + INIT)
                            nc.tensor.matmul(HA[:, :], w[:, m * D:(m + 1) * D], h2T[:, :], start=True, stop=True
                                             ).then_inc(h1_ps, 1)
                            if m == 0:
                                pe.wait_ge(m0_ready, kk * MH + INIT)
                            nc.tensor.matmul((HBk, HC)[m][:, :], w[:, H + m * D:H + (m + 1) * D], h2T[:, :],
                                             start=True, stop=True).then_inc(h11_ps, 1)
                        if pr is not None:
                            pair(i, pr + m)
                        if prev:
                            second(kk - 2, n - 1, slot, m)

                with pe.Fori(0, BODIES) as i:
                    for j in range(PER):
                        expert(q * NE + i * PER + (j + SHARED) if ffn else None,
                               q * (NE // 2) + i * 2 + (2 + j // 2), j % 2, ffn, i, 2 * j if scan else None)
                    if scan:
                        readout(i, PAIRS - 1)
                if scan:
                    pe.wait_ge(yg_ready, s + 1)
                    if ffn:
                        pe.wait_ge(hb_ready, s * NE * MH + INIT)
                    for j in range(CT):
                        mm = nc.tensor.matmul(HA[:, j * D:(j + 1) * D], ygT[:, j * D:(j + 1) * D], cst("wout"),
                                              start=True, stop=True)
                    mm.then_inc(o_ps, 1)
                if ffn:
                    for slot in range(2):
                        for m in range(MH):
                            second(s * NE - 2 + slot, s * (NE // 2), slot, m, slot == 1 and m == MH - 1)
                    pe.wait_ge(yT_ready, s)
                    pe.wait_ge(m0_ready, s * NE * MH + INIT)
                    for j in range(CT):
                        mm = nc.tensor.transpose(HC[:, j * D:(j + 1) * D], yT[:, j * D:(j + 1) * D], ident)
                    mm.then_inc(yt_ps, 1)
                if scan:
                    pe.wait_ge(h2_ready, s + 1)
                    for j in range(CT):
                        mm = nc.tensor.transpose(HBk[:, j * D:(j + 1) * D], Hn[0][:, j * D:(j + 1) * D], ident)
                    mm.then_inc(h2T_ps, 1)
                    pe.wait_ge(h2T_ready, s + 1)
                    pe.wait_ge(dtc_ready, (s + 1) * (TC // 2) + 2)
                    for j in range(CT):
                        mm = nc.tensor.matmul(DTB[:, j * E:(j + 1) * E], h2T[:, j * D:(j + 1) * D], cst("wg"),
                                              start=True, stop=True)
                    mm.then_inc(lg_ps, 1)
                    for k in range(SHARED):
                        expert(s * NE + k, s * (NE // 2) + 1, k, False, 0, None)
                    pe.wait_ge(gt_ready, s + 1)
                    for j in range(CT):
                        mm = nc.tensor.transpose(DTB[0:E, j * D:(j + 1) * D], gt[:, j * E:(j + 1) * E], ident)
                    mm.then_inc(gT_ps, 1)
                    pe.wait_ge(gT_ready, s + 1)
                    nc.tensor.matmul(YACC[:, :], b2_sb[:, :], gT[:, :], start=True, stop=False,
                                     skip_group_check=True)

            stage(0, True, False)
            with pe.Fori(1, NC) as s:
                stage(s, True, True)
            stage(NC, False, True)

        @block.scalar
        def _(act):
            for started in (hT_ready, z_ready, hb_ready, th1_ready, dte_ready, *part_ready):
                act.sem_inc(started, INIT)
            act.wait_ge(ld_w, 48)
            nc.scalar.activation(sct[:, :], cst("ct"), ACT.Silu).then_inc(sct_ready, 1)

            with act.Fori(0, NC // 2) as c2:
                for u in range(2):
                    c = c2 * 2 + u
                    act.wait_ge(hT_ps, c + 1 + INIT)
                    nc.scalar.copy(hT[u][:, :], HA[:, :]).then_inc(hT_ready, 1)
                    act.wait_ge(inp_ps, c * 2 + 1)
                    if u == 0:
                        act.wait_ge(pool_const, 5)
                    nc.scalar.activation(XC[:, bass.ds(c * CW + XPAD * B, CW)], HBk[:, :], ACT.Identity,
                                         bias=col(IN_B)).then_inc(xc_ready, 1)
                    act.wait_ge(inp_ps, c * 2 + 2)
                    nc.scalar.activation(ZG[:, bass.ds(c * CW, CW)], HC[:, :], ACT.Silu,
                                         bias=col(IN_B + 1)).then_inc(z_ready, 1)
            for h in range(2):
                v = XS[:, h * T * B // 2:(h + 1) * T * B // 2]
                act.wait_ge(conv_done, h + 1)
                nc.scalar.activation(v, v, ACT.Silu).then_inc(xs_ready, 1)

            act.wait_ge(bc_ps, 1)
            for half, bnk in enumerate((HA, HBk)):
                nc.scalar.activation(BCOL[:, half * (T + GT):half * (T + GT) + T], bnk[:, :], ACT.Identity, bias=col(B_B))
            cv = CBLK[:, :].rearrange("p (t h b) -> p t h b", h=2, b=HB)
            for half, bnk in enumerate((HC, DTB)):
                for b in range(HB):
                    r = slice(N * b, N * b + N)
                    last = nc.scalar.activation(cv[r, :, half, b], bnk[r, :], ACT.Identity,
                                                bias=wc_sb[r, c0 + C_B:c0 + C_B + 1])
            last.then_inc(bcol_ready, 1)

            act.wait_ge(const_ready, 1)
            nc.scalar.activation(arep[:, :], arep[:, :], ACT.Exp).then_inc(aexp_ready, 1)
            with act.Fori(0, NC // 2) as c2:
                for u in range(2):
                    c = c2 * 2 + u
                    nc.scalar.copy(hT[u][:, :], XS[:, bass.ds(c * CW, CW)]).then_inc(xst_ready, 1)
                    act.wait_ge(dti_ready, c + 1)
                    nc.scalar.activation(dte[:, :], dti[:, :], ACT.Exp).then_inc(dte_ready, 1)
                    act.wait_ge(dte_ready, c + 1 + INIT)
                    nc.scalar.activation(dtl[:, :], dte[:, :], ACT.Ln, bias=col(ONE)).then_inc(dtl_ready, 1)
                    part = PB[u][:, :].rearrange("p (m f) -> p m f", m=PARTS)
                    act.wait_ge(du_ready, c + 1 + INIT)
                    act.wait_ge(ds_stored[u], c2 * (STORES * 16) + 16 * INIT)
                    nc.scalar.copy(part[:, 0, :], DU[u][:, :]).then_inc(part_ready[u], 1)
                    act.wait_ge(res_ready, c * 2 + 1)
                    nc.scalar.copy(part[:, 1, :], res1[:, :]).then_inc(part_ready[u], 1)
                    act.wait_ge(res_ready, c * 2 + 2)
                    nc.scalar.copy(part[:, 2, :], res2[:, :]).then_inc(part_ready[u], 1)

            def copy_dt(p, slot):
                act.wait_ge(dt_bc, p + 1)
                nc.scalar.copy(dtc[slot][:, :], DTB[:, :]).then_inc(dtc_ready, 1)

            def exp_dta(p, slot):
                act.wait_ge(dta_ready, p + 1)
                nc.scalar.activation(ab[slot][:, :], dta[slot][:, :], ACT.Exp).then_inc(a_ready, 1)

            copy_dt(0, 0)
            copy_dt(1, 1)
            exp_dta(0, 0)

            def stage(s, scan, ffn):
                q = s - 1

                def copy_ahead(i, n):
                    p = s * (TC // 2) + i * PAIRS + n
                    act.wait_ge(dta_ready, p + 1)
                    copy_dt(p + 2, n % 2)

                def exp_ahead(i, n):
                    p = s * (TC // 2) + i * PAIRS + n
                    act.wait_ge(p_done, p * 2 + INIT)
                    exp_dta(p + 1, (n + 1) % 2)

                def pre(kk, slot, m):
                    act.wait_ge(h1_ps, kk * MH + (m + 1))
                    nc.scalar.activation(hb[slot][:, m * CW:(m + 1) * CW], HA[:, :], ACT.Identity,
                                         bias=W1S[slot][:, 2 * H + m:2 * H + m + 1]).then_inc(hb_ready, 1)

                def tanh(kk, slot):
                    act.wait_ge(hb_ready, kk * MH + MH + INIT)
                    act.wait_ge(th1_ready, kk + INIT)
                    nc.scalar.activation(th[:, :], hb[slot][:, :], ACT.Tanh, scale=0.5).then_inc(th_ready, 1)

                def one_plus(kk, slot):
                    act.wait_ge(th_ready, kk + 1)
                    act.wait_ge(wg_ready, kk - 1 + INIT)
                    nc.scalar.activation(th1[slot][:, :], th[:, :], ACT.Identity, bias=col(ONE)
                                         ).then_inc(th1_ready, 1)

                with act.Fori(0, BODIES) as i:
                    for j in range(PER):
                        kk, slot = q * NE + i * PER + (j + SHARED), j % 2
                        for m in range(MH):
                            if ffn:
                                pre(kk, slot, m)
                            if scan:
                                exp_ahead(i, 2 * j + m)
                            if ffn and m:
                                tanh(kk, slot)
                            if scan:
                                copy_ahead(i, 2 * j + m)
                        if ffn:
                            one_plus(kk, slot)
                if ffn:
                    act.wait_ge(w2_done, s * NE + INIT)
                    nc.scalar.activation(yT[:, :], YACC[:, :], ACT.Identity, bias=col(BS2)).then_inc(yT_ready, 1)
                if scan:
                    act.wait_ge(h2T_ps, s + 1)
                    nc.scalar.copy(h2T[:, :], HBk[:, :]).then_inc(h2T_ready, 1)
                    for k in range(SHARED):
                        kk = s * NE + k
                        pre(kk, k, 0)
                        if k == 0:
                            act.wait_ge(lgd_ready, s + 1)
                            nc.scalar.activation(ex[:, :], rp[:, :], ACT.Exp).then_inc(ex_ready, 1)
                        pre(kk, k, 1)
                        tanh(kk, k)
                        one_plus(kk, k)
                    act.wait_ge(gT_ps, s + 1)
                    nc.scalar.copy(gT[:, :], DTB[0:E, :]).then_inc(gT_ready, 1)

            stage(0, True, False)
            with act.Fori(1, NC) as s:
                stage(s, True, True)
            stage(NC, False, True)

        @block.vector
        def _(dve):
            for started in (du_ready, s_done, p_done, q_done, m0_ready):
                dve.sem_inc(started, INIT)
            own = Chain(dve, dve_own)
            V = nc.vector
            dve.wait_ge(ld_w, 48)
            own(V.tensor_copy(sel_bf[:, :], cst("sel")[0:ROWS, :]))
            own(V.memset(S[SR - 1][:, :], 0.0))
            own(V.tensor_scalar(arep[:, :], cst("arep"), -5.0, 2.0, ALU.max, ALU.min))
            own(V.tensor_scalar(b2_sb[:, :], b2_sb[:, :], 2.0, None, ALU.mult))
            own.wait()
            nc.vector.engine_nop().then_inc(const_ready, 1)
            dve.wait_ge(mod_ps, 1)
            own(V.tensor_copy(mods[:, 0:3 * D], HA[:, 0:3 * D]))
            own(V.tensor_copy(mods[:, 3 * D:6 * D], HBk[:, 0:3 * D]))
            own.wait()
            for m in (CA, CB):
                own(V.tensor_scalar(m, m, 1.0, None, ALU.add))
            for i, g in enumerate((GA, GB)):
                own(V.scalar_tensor_tensor(out=gmag[:, i * D:(i + 1) * D], in0=g, scalar=-1.0, in1=g,
                                           op0=ALU.mult, op1=ALU.max))
                own(V.tensor_scalar(gsgn[:, i * D:(i + 1) * D], g, 0.0, 2.0, ALU.is_ge, ALU.mult))
            own.wait()
            own(V.tensor_scalar(gmag[:, :], gmag[:, :], 0.25, None, ALU.max))
            own.wait()
            for i, g in enumerate((GA, GB)):
                own(V.scalar_tensor_tensor(out=g, in0=gsgn[:, i * D:(i + 1) * D], scalar=-1.0,
                                           in1=gmag[:, i * D:(i + 1) * D], op0=ALU.add, op1=ALU.mult))
            own.wait()
            own(V.tensor_tensor(gg[:, :], GA, cst("lng"), ALU.mult))
            own(V.tensor_tensor(gbias[:, :], GA, cst("lnb"), ALU.mult))
            own.wait()
            V.engine_nop().then_inc(mod_ready, 1)

            def normalise(dst, src, n):
                for j in range(CT):
                    own(V.bn_stats(st[:, 6 * j:6 * j + 6], src(j)))
                own.wait()
                s3 = st[:, :].rearrange("p (j k) -> p j k", k=6)
                own(V.tensor_tensor(mean[:, :], s3[:, :, 1], s3[:, :, 4], ALU.add))
                own(V.tensor_tensor(mdif[:, :], s3[:, :, 1], s3[:, :, 4], ALU.subtract))
                own(V.tensor_tensor(vsum[:, :], s3[:, :, 2], s3[:, :, 5], ALU.add))
                own.wait()
                own(V.tensor_scalar(mean[:, :], mean[:, :], 0.5, None, ALU.mult))
                own(V.tensor_tensor(mdif[:, :], mdif[:, :], mdif[:, :], ALU.mult))
                own(V.tensor_scalar(vsum[:, :], vsum[:, :], 1.0 / D, EPS, ALU.mult, ALU.add))
                own.wait()
                V.scalar_tensor_tensor(out=vareps[:, :], in0=mdif[:, :], scalar=0.25, in1=vsum[:, :],
                                       op0=ALU.mult, op1=ALU.add).then_inc(var_ready, 1)
                dve.wait_ge(rstd_ready, n + 1)
                for j in range(CT):
                    own(V.tensor_scalar(dst[:, j * D:(j + 1) * D], src(j), mean[:, j:j + 1],
                                        rstd[:, j:j + 1], ALU.subtract, ALU.mult))
                own.wait()

            def by_feature(dst, a, b, op):
                return V.tensor_tensor(tiles(dst), tiles(a), over_tiles(b), op)

            dve.wait_ge(ld_x, 16)
            start, per = own.n, 2 * (2 * CT + 7)
            with dve.Fori(0, NC // 2) as c2:
                own.at(c2 * per + start)
                for u in range(2):
                    c = c2 * 2 + u
                    dve.wait_ge(hT_ps, c + INIT)
                    dve.wait_ge(hr_done, c + INIT)
                    normalise(Hn[u], lambda j: X[:, bass.ds(c * CW + j * D, D)], c)
                    own(by_feature(Hn[u][:, :], Hn[u][:, :], CA, ALU.mult))
                    own.wait()
                    by_feature(Hn[u][:, :], Hn[u][:, :], SA, ALU.add).then_inc(h_ready, 1)
                assert own.n == per
            own.at(start + NC // 2 * per)

            dve.wait_ge(xc_ready, NC)
            half = T * B // 2
            for h in range(2):
                def tap(k):
                    return XC[:, h * half + k * B:h * half + k * B + half]

                y = XS[:, h * half:(h + 1) * half]
                own(V.tensor_scalar(y, tap(0), col(CONV_W), col(CONV_B), ALU.mult, ALU.add))
                for k in range(1, KW):
                    own.wait()
                    ins = V.scalar_tensor_tensor(out=y, in0=tap(k), scalar=col(CONV_W + k), in1=y,
                                                 op0=ALU.mult, op1=ALU.add)
                    if k < KW - 1:
                        own(ins)
                ins.then_inc(conv_done, 1)

            with dve.Fori(0, NC // 2) as c2:
                for u in range(2):
                    c = c2 * 2 + u
                    dve.wait_ge(dt_ps, c + 1)
                    dve.wait_ge(dte_ready, c + INIT)
                    by_feature(dti[:, :], U0[:, :], cst("dtb"), ALU.add).then_inc(dti_ready, 1)
                    dve.wait_ge(dtl_ready, c + 1)
                    dve.wait_ge(part_ready[u], c2 * PARTS + INIT)
                    V.tensor_scalar(DU[u][:, 0:CW], dtl[:, :], 0.001, 0.2, ALU.max, ALU.min
                                    ).then_inc(dt_clipped, 1)
                    dve.wait_ge(dt_clipped, c + 1)
                    V.tensor_tensor(DU[u][:, CW:2 * CW], DU[u][:, 0:CW], U1[:, :], ALU.mult
                                    ).then_inc(du_ready, 1)
            dve.wait_ge(aexp_ready, 1)
            V.tensor_scalar(arep[:, :], arep[:, :], -1.0, None, ALU.mult).then_inc(arep_ready, 1)
            dve.wait_ge(bcol_ready, 1)
            b3 = BCOL[:, :].rearrange("p (h t) -> p h t", h=2)
            own(V.memset(b3[:, :, T:T + GT], 0.0))

            def group_scalars(g, slot):
                V.tensor_copy(BNOW[slot][:, :].rearrange("p (h t) -> p h t", h=2),
                              b3[:, :, bass.ds(g * GT, GT)]).then_inc(b_ready, 1)

            own.wait()
            group_scalars(0, 0)
            per_stage = 4 * CT + 33

            def stage(s, scan, ffn):
                q = s - 1

                def step(i, n, h):
                    p = s * (TC // 2) + i * PAIRS + n
                    t = s * TC + i * (2 * PAIRS) + (2 * n + h)
                    now, prev = S[(2 * n + h) % SR], S[(2 * n + h - 1) % SR]
                    if h == 0:
                        dve.wait_ge(a_ready, p + 1)
                        dve.wait_ge(u_bc, p + 1)
                        dve.wait_ge(y_done, t + 2)
                        if n % 4 == 0:
                            dve.wait_ge(b_ready, s * (TC // GT) + i * 2 + (n // 4 + 1))
                    dve.wait_ge(s_done, t + INIT)
                    V.tensor_tensor(pt[:, :], prev[:, :], ab[n % 2][:, h * SW:(h + 1) * SW], ALU.mult
                                    ).then_inc(p_done, 1)
                    if n % 4 == 2 and h == 0:
                        group_scalars(s * (TC // GT) + i * 2 + (n // 4 + 1), 1 - n // 4)
                    dve.wait_ge(p_done, t + 1 + INIT)
                    for half in range(2):
                        k = half * GT + 2 * n % GT + h
                        r = slice(half * D, (half + 1) * D)
                        V.scalar_tensor_tensor(out=qt[:, r], in0=U[n % 2][:, h * SW + half * D:h * SW + (half + 1) * D],
                                               scalar=BNOW[n // 4][:, k:k + 1], in1=pt[:, r],
                                               op0=ALU.mult, op1=ALU.add).then_inc(q_done, 1)
                    dve.wait_ge(q_done, t * 2 + 2 + INIT)
                    V.tensor_scalar(now[:, :], qt[:, :], 10.0, -10.0, ALU.min, ALU.max).then_inc(s_done, 1)

                def gate(kk, slot, m):
                    dve.wait_ge(hb_ready, kk * MH + (m + 1) + INIT)
                    dve.wait_ge(h11_ps, kk * MH + (m + 1))
                    if m == 0:
                        dve.wait_ge(hh_ready, kk - 1 + INIT)
                    r = slice(m * CW, (m + 1) * CW)
                    V.scalar_tensor_tensor(out=m0[slot][:, r], in0=(HBk, HC)[m][:, :],
                                           scalar=W1S[slot][:, 2 * H + MH + m:2 * H + MH + m + 1],
                                           in1=hb[slot][:, r], op0=ALU.add, op1=ALU.mult).then_inc(m0_ready, 1)

                if ffn:
                    own.at(q * per_stage + before)
                with dve.Fori(0, BODIES) as i:
                    for j in range(PER):
                        kk = q * NE + i * PER + (j + SHARED)
                        if scan:
                            step(i, 2 * j, 0)
                            step(i, 2 * j, 1)
                        if ffn:
                            gate(kk, j % 2, 0)
                        if scan:
                            step(i, 2 * j + 1, 0)
                            step(i, 2 * j + 1, 1)
                        if ffn:
                            gate(kk, j % 2, 1)
                if scan:
                    cols = bass.ds(s * CW, CW)
                    dve.wait_ge(y_done, (s + 1) * TC + SR)
                    V.tensor_tensor(ygT[:, :], YSC[:, :], ZG[:, cols], ALU.mult).then_inc(yg_ready, 1)
                    dve.wait_ge(o_ps, s + 1)
                    own(V.tensor_tensor(om[:, :], HA[:, :], HR[:, cols], ALU.add))
                    own.wait()
                    normalise(om, lambda j: om[:, j * D:(j + 1) * D], s * 2 + NC)
                    own(by_feature(om[:, :], om[:, :], gg[:, :], ALU.mult))
                    own.wait()
                if ffn:
                    dve.wait_ge(yt_ps, s)
                    dve.wait_ge(stored, q * 16 + 16 * INIT)
                    own(by_feature(O[:, :], HC[:, :], GB, ALU.mult))
                    own.wait()
                    V.tensor_tensor(O[:, :], O[:, :], X2[:, :], ALU.add).then_inc(out_ready, 1)
                if scan:
                    if ffn:
                        dve.wait_ge(out_ready, s)
                    own(V.tensor_tensor(X2[:, :], om[:, :], X[:, cols], ALU.add))
                    own.wait()
                    normalise(Hn[0], lambda j: X2[:, j * D:(j + 1) * D], s * 2 + (NC + 1))
                    own(by_feature(Hn[0][:, :], Hn[0][:, :], CB, ALU.mult))
                    own.wait()
                    by_feature(Hn[0][:, :], Hn[0][:, :], SB, ALU.add).then_inc(h2_ready, 1)

                    def e3(ap):
                        return ap.rearrange("p (j e) -> p j e", e=E)

                    def over_e(ap):
                        return ap.unsqueeze(2).broadcast_to([P, CT, E])

                    order = cst("order").unsqueeze(1).broadcast_to([P, CT, E])
                    dve.wait_ge(lg_ps, s + 1)
                    own(V.tensor_copy(lg[:, :], DTB[:, 0:CT * E]))
                    own.wait()

                    def first_largest(top, src, pick):
                        own(V.tensor_reduce(top, e3(src), AX.X, ALU.max))
                        own.wait()
                        own(V.tensor_tensor(e3(pick), e3(src), over_e(top), ALU.is_equal))
                        own.wait()
                        own(V.tensor_tensor(e3(pick), e3(pick), order, ALU.mult))
                        own.wait()
                        own(V.tensor_reduce(place[:, :], e3(pick), AX.X, ALU.max))
                        own.wait()
                        own(V.tensor_tensor(e3(pick), e3(pick), over_e(place[:, :]), ALU.is_equal))
                        own.wait()

                    first_largest(top[:, :], lg[:, :], pick1[:, :])
                    V.tensor_tensor(e3(rp[:, :]), e3(lg[:, :]), over_e(top[:, :]), ALU.subtract
                                    ).then_inc(lgd_ready, 1)
                    gate(s * NE, 0, 0)
                    own(V.scalar_tensor_tensor(out=lg[:, :], in0=pick1[:, :], scalar=-1e38, in1=lg[:, :],
                                               op0=ALU.mult, op1=ALU.add))
                    own.wait()
                    first_largest(top2[:, :], lg[:, :], pick2[:, :])
                    gate(s * NE, 0, 1)
                    own(V.tensor_tensor(pick1[:, :], pick1[:, :], pick2[:, :], ALU.add))
                    own.wait()
                    dve.wait_ge(ex_ready, s + 1)
                    own(V.tensor_tensor(ex[:, :], ex[:, :], pick1[:, :], ALU.mult))
                    own.wait()
                    own(V.tensor_reduce(gsum[:, :], e3(ex[:, :]), AX.X, ALU.add))
                    own.wait()
                    own(V.reciprocal(grec[:, :], gsum[:, :]))
                    own.wait()
                    V.scalar_tensor_tensor(out=e3(gt[:, :]), in0=e3(ex[:, :]), scalar=0.5, in1=over_e(grec[:, :]),
                                           op0=ALU.mult, op1=ALU.mult).then_inc(gt_ready, 1)
                    for k in range(1, SHARED):
                        for m in range(MH):
                            gate(s * NE + k, k, m)

            stage(0, True, False)
            before = own.base + own.n
            with dve.Fori(1, NC) as s:
                stage(s, True, True)
                assert own.n == per_stage, own.n
            stage(NC, False, True)


def kernel(**inputs):
    import numpy as np
    import concourse.bacc as bacc
    from concourse.bass_utils import run_bass_kernel_spmd

    g = {k: np.asarray(v) for k, v in inputs.items()}

    def a(name):
        return g["L0_attn_" + name]

    def f(name):
        return g["L0_ffn_" + name]

    def row(v):
        return np.broadcast_to(v[None, :], (P, v.shape[0]))

    def hidden_cols(v):
        return v.reshape(MH, P).T

    d = D
    sel = np.zeros((P, P), np.float32)
    for r in range(ROWS):
        sel[r, N * (r % HB):N * (r % HB) + N] = 1.0
    cols = np.zeros((P, 16), np.float32)
    cols[:, 0:2] = a("in_proj_b").reshape(2, d).T
    cols[:, 2:6] = a("conv_w")[:, 0, :]
    cols[:, 6] = a("conv_b")
    cols[:, 7] = np.tile(a("B_b"), HB)
    cols[:, 8] = np.tile(a("C_b"), HB)
    cols[:, 9] = f("bs2")
    cols[:, 10] = 1.0
    wcol = np.concatenate([
        a("in_proj_w").T, a("dt_w").T, a("B_w").T, a("C_w").T, a("out_w").T, f("Wg"),
        np.tile(a("A_log").T, (HB, 1)), np.eye(P, dtype=np.float32), np.tile(g["L0_c"].T, (1, TT)), cols,
        row(a("dt_b")), row(a("out_b")), row(a("ln_g")), row(a("ln_beta")), sel,
        row(np.arange(E, 0, -1).astype(np.float32)),
    ], axis=1)
    w1s = [np.concatenate([f("Ws1")[:, k * H:(k + 1) * H], f("Ws11")[:, k * H:(k + 1) * H],
                           hidden_cols(f("bs1")[k * H:(k + 1) * H]), hidden_cols(f("bs11")[k * H:(k + 1) * H])], axis=1)
           for k in range(SHARED)]
    w1r = [np.concatenate([f("W1")[e], f("W11")[e], hidden_cols(f("b1")[e]), hidden_cols(f("b11")[e])], axis=1)
           for e in range(E)]

    def second(w):
        return w.reshape(MH, P, D).transpose(1, 0, 2).reshape(P, MH * D)

    w2s = [second(f("Ws2")[k * H:(k + 1) * H]) for k in range(SHARED)] + [second(f("W2")[e]) for e in range(E)]
    nt = T // TT
    xt = a("x").reshape(B, nt, TT, D).transpose(2, 0, 1, 3).reshape(P, nt * D)
    arrays = {
        "in_x": xt, "in_wcol": wcol, "in_wmod": g["L0_wmod"], "in_w1": np.stack(w1s + w1r),
        "in_w2": np.stack(w2s), "in_b2": f("b2"),
    }
    arrays = {k: np.ascontiguousarray(v) for k, v in arrays.items()}
    nc = bacc.Bacc("TRN2", target_bir_lowering=False, num_devices=1)
    aps = {k: nc.dram_tensor(k, v.shape, mybir.dt.from_np(v.dtype), kind="ExternalInput").ap()
           for k, v in arrays.items()}
    out = nc.dram_tensor("out_0", (P, nt * D), F32, kind="ExternalOutput").ap()
    build(nc, aps["in_x"], aps["in_wcol"], aps["in_wmod"], aps["in_w1"], aps["in_w2"], aps["in_b2"], out)
    r = run_bass_kernel_spmd(nc, [arrays], core_ids=[0])
    y = r.results[0]["out_0"]
    return y.reshape(TT, B, nt, D).transpose(1, 2, 0, 3).reshape(B, T, D)
```

```python
from contextlib import ExitStack

import concourse.bass as bass
from concourse import mybir

F32 = mybir.dt.float32
BF16 = mybir.dt.bfloat16
F32R = mybir.dt.float32r
ALU = mybir.AluOpType
ACT = mybir.ActivationFunctionType
AX = mybir.AxisListType

B, T, D, N = 8, 512, 128, 32
E, H, HS = 16, 256, 512
P = 128
TT = P // B
TC = 64
NC = T // TC
CT = TC // TT
CW = TC * B
HB = B // 2
GT = 8
PARTS = 3
ROWS = PARTS * HB
SW = 2 * D
GW = 2 * GT * SW
SHARED = HS // H
NE = SHARED + E
MH = H // P
W1W = 4 * H
PER = 4
PAIRS = 2 * PER
BODIES = E // PER
EPS = 1e-5
GP = 416
GP_LAST = 128
XPAD = 2
KW = 4
LAG = 3
INIT = 2


class Chain:

    def __init__(self, eng, sem):
        self.eng, self.sem, self.base, self.n = eng, sem, 0, 0

    def at(self, base):
        self.base, self.n = base, 0

    def __call__(self, ins):
        ins.then_inc(self.sem, 1)
        self.n += 1

    def wait(self, but=0):
        self.eng.wait_ge(self.sem, self.base + (self.n - but))


def build(nc, x, wcol, wmod, w1, w2, b2, out):
    with ExitStack() as ctx:
        def sb(name, cols, dt=F32, parts=P):
            return ctx.enter_context(nc.sbuf_tensor(name, [parts, cols], dt))

        def bank(name):
            return ctx.enter_context(nc.psum_tensor(name, [P, 512], F32))

        def sem(name):
            return ctx.enter_context(nc.semaphore(name))

        names = dict(win=2 * D, wdt=D, wb=N, wc=N, wout=D, wg=E, arep=D, ident=D, ct=P, cols=16,
                     dtb=D, outb=D, lng=D, lnb=D, sel=P, order=E, bs2=D)
        at, o = {}, 0
        for k, v in names.items():
            at[k] = (o, o + v)
            o += v
        wc_sb = sb("wc_sb", o)

        def cst(name):
            a, b = at[name]
            return wc_sb[:, a:b]

        c0 = at["cols"][0]

        def col(i):
            return wc_sb[:, c0 + i:c0 + i + 1]

        IN_B, CONV_W, CONV_B, B_B, C_B, ONE = 0, 2, 6, 7, 8, 9
        sct = sb("sct", P)
        spread_bf = sb("spread_bf", P, BF16, ROWS)
        b2_sb = sb("b2_sb", D, F32, E)
        mods = sb("mods", 6 * D)
        SA, CA, GA, SB, CB, GB = (mods[:, i * D:(i + 1) * D] for i in range(6))
        arep = sb("arep", D)
        gg = sb("gg", D)
        gbias = sb("gbias", D)
        mexp = sb("mexp", CT)

        X = sb("X", T * B * D // P)
        HR = sb("HR", T * B * D // P)
        ZG = sb("ZG", T * B)
        XC = sb("XC", (T + KW - 1) * B)
        XS = sb("XS", T * B)
        BCOL = sb("BCOL", 2 * (T + GT))
        BNOW = [sb(f"BNOW{i}", 2 * GT) for i in range(2)]
        CBLK = sb("CBLK", T * B)
        XTOK = CBLK

        st = sb("st", CT * 6)
        mean, mdif, vsum = (sb(n, CT) for n in ("mean", "mdif", "vsum"))
        vareps = sb("vareps", CT)
        rstd = sb("rstd", CT)
        Hn = [sb(f"Hn{i}", CW) for i in range(2)]
        hT = [sb(f"hT{i}", CW) for i in range(2)]
        dti = sb("dti", CW)
        dte = sb("dte", CW)
        rows = sb("rows", CW)
        half_gate = rows[32:32 + SHARED, :]
        DU = [sb(f"DU{i}", 2 * CW) for i in range(2)]
        res1 = sb("res1", 2 * CW)
        res2 = sb("res2", 2 * CW)
        wmod_sb = res1[:, 0:6 * D]
        gmag, gsgn = res2[:, 0:2 * D], res2[:, 2 * D:4 * D]
        PB = [sb(f"PB{i}", PARTS * 2 * CW, BF16) for i in range(2)]
        R = [sb(f"R{i}", GW, BF16, ROWS) for i in range(2)]
        dtc = [sb(f"dtc{i}", 2 * SW) for i in range(2)]
        dta = [sb(f"dta{i}", 2 * SW) for i in range(2)]
        ab = [sb(f"ab{i}", 2 * SW) for i in range(2)]
        SR = 8
        S = [sb(f"S{i}", SW) for i in range(SR)]
        pt = sb("pt", SW)
        qt = sb("qt", SW)
        W1S = [sb(f"W1S{i}", W1W) for i in range(2)]
        W1B = [sb(f"W1B{i}", 2 * MH) for i in range(2)]
        WIN = [t[:, :].bitcast(F32)[:, 0:2 * H] for t in PB]
        XR = sb("XR", 2 * CW)
        W2S = [sb(f"W2S{i}", MH * D) for i in range(2)]
        GS = [dti, dte]
        hid = [t[:, i * MH * CW:(i + 1) * MH * CW] for t in (XS, XC) for i in range(4)]
        hb, th1, m0, th, wg_ = hid[0:2], hid[2:4], hid[4:6], hid[6], hid[7]
        hh = DU
        ygT = hT[0]
        om, X2, O = hT[0], res1[:, CW:2 * CW], res2[:, 0:CW]
        REST = [res1, res2]
        X2n = Hn[1]
        h2T = hT[1]
        lg, pick1, pick2, rp, ex, gt = (res1[:, i * CT * E:(i + 1) * CT * E] for i in range(6))
        top, top2, place = (sb(n, CT) for n in ("top", "top2", "place"))
        gsum = sb("gsum", CT)
        grec = sb("grec", CT)
        gT, yT = rows[0:E, :], res2[:, CW:2 * CW]

        YACC, YSC, DTB, U0, U1, HA, HBk, HC = (
            bank(n) for n in ("YACC", "YSC", "DTB", "U0", "U1", "HA", "HBk", "HC"))
        U = [U0, U1]

        DS = nc.dram_tensor("scan_rows", ((T // TT + 1) * P, PARTS * 2 * D), BF16).ap()
        WR = nc.dram_tensor("w1_parts", (NE * P, W1W), F32).ap()
        GD = nc.dram_tensor("gate_rows", (NE, CW), F32).ap()

        ld_x, ld_w = sem("ld_x"), sem("ld_w")
        dve_own = sem("dve_own")
        pool_const = sem("pool_const")
        sct_ready, mod_ps, mod_ready = sem("sct_ready"), sem("mod_ps"), sem("mod_ready")
        var_ready, rstd_ready = sem("var_ready"), sem("rstd_ready")
        h_ready, hr_done, xg_done = sem("h_ready"), sem("hr_done"), sem("xg_done")
        hT_ps, hT_ready, inp_ps, xc_ready, z_ready = (
            sem(n) for n in ("hT_ps", "hT_ready", "inp_ps", "xc_ready", "z_ready"))
        conv_done, xs_ready, bc_ps, bcol_ready = (
            sem(n) for n in ("conv_done", "xs_ready", "bc_ps", "bcol_ready"))
        xst_ready, dt_ps, dti_ready, dte_ready, dtl_ready, du_ready = (
            sem(n) for n in ("xst_ready", "dt_ps", "dti_ready", "dte_ready", "dtl_ready", "du_ready"))
        part_ready = [sem(f"part_ready{i}") for i in range(2)]
        ds_stored = [[sem(f"ds_stored{i}_{m}") for m in range(PARTS)] for i in range(2)]
        x2_ready, x2_kept = sem("x2_ready"), sem("x2_kept")
        w_loaded = [sem(f"w_loaded{i}") for i in range(2)]
        wr_stored = [sem(f"wr_stored{i}") for i in range(2)]
        w_high, w_split, xh_ready, xr_ready = (sem(n) for n in ("w_high", "w_split", "xh_ready", "xr_ready"))
        c_zero, c_ready = sem("c_zero"), sem("c_ready")
        xt_ps, xtok_ready = sem("xt_ps"), sem("xtok_ready")
        rest_ready = sem("rest_ready")
        last_ready = [sem(f"last_ready{i}") for i in range(2)]
        r_loaded = [sem(f"r_loaded{i}") for i in range(2)]
        dt_bc, u_bc, dtc_ready, dta_ready, a_ready = (
            sem(n) for n in ("dt_bc", "u_bc", "dtc_ready", "dta_ready", "a_ready"))
        p_done, q_done, s_done, y_done = (sem(n) for n in ("p_done", "q_done", "s_done", "y_done"))
        w1_loaded = [sem(f"w1_loaded{i}") for i in range(2)]
        w2_loaded = [sem(f"w2_loaded{i}") for i in range(2)]
        g_loaded = [sem(f"g_loaded{i}") for i in range(2)]
        h1_ps, h11_ps, hb_ready, th_ready, th1_ready = (
            sem(n) for n in ("h1_ps", "h11_ps", "hb_ready", "th_ready", "th1_ready"))
        m0_ready, wg_ready, wg1_ready, hh_ready, w2_done = (
            sem(n) for n in ("m0_ready", "wg_ready", "wg1_ready", "hh_ready", "w2_done"))
        yg_ready, o_ps, h2_ready, h2T_ps, h2T_ready, lg_ps = (
            sem(n) for n in ("yg_ready", "o_ps", "h2_ready", "h2T_ps", "h2T_ready", "lg_ps"))
        lgd_ready, ex_ready, gt_ready, gT_ps, gT_ready, gd_stored = (
            sem(n) for n in ("lgd_ready", "ex_ready", "gt_ready", "gT_ps", "gT_ready", "gd_stored"))
        const_ready, aexp_ready, arep_ready = sem("const_ready"), sem("aexp_ready"), sem("arep_ready")
        zero_rows, dt_clipped = sem("zero_rows"), sem("dt_clipped")
        yT_ready, yt_ps, out_ready, stored = (
            sem(n) for n in ("yT_ready", "yt_ps", "out_ready", "stored"))

        def tiles(ap, w=D):
            return ap.rearrange("p (j d) -> p j d", d=w)

        def over_tiles(ap, n=CT):
            return ap.unsqueeze(1).broadcast_to([P, n, D])

        block = ctx.enter_context(nc.Block())

        @block.sync
        def _(sp):
            for x_stored in (*ds_stored[0], *ds_stored[1], *wr_stored, stored):
                sp.sem_inc(x_stored, 16 * INIT)
            sp.dma_start(wc_sb[:, :], wcol).then_inc(ld_w, 16)
            sp.dma_start(wmod_sb[:, :], wmod).then_inc(ld_w, 16)
            sp.dma_start(b2_sb[:, :], b2).then_inc(ld_w, 16)
            sp.dma_start(X[:, :], x).then_inc(ld_x, 16)

            sp.wait_ge(pool_const, 1)
            zeros = S[0][:, :].bitcast(BF16)[:, 0:2 * D]
            for m in range(PARTS):
                sp.dma_start(DS[T * B:T * B + P, m * 2 * D:(m + 1) * 2 * D], zeros).then_inc(zero_rows, 16)

            def load_whole(k, slot):
                sp.dma_start(WIN[slot], w1[bass.ds(k, 1), :, 0:2 * H].rearrange("a p f -> (a p) f")
                             ).then_inc(w_loaded[slot], 16)

            def store_split(k, slot):
                sp.wait_ge(w_split, k + 1)
                sp.dma_start(WR[bass.ds(k * P, P), :], W1S[slot][:, :]).then_inc(wr_stored[slot], 16)

            for k in range(2):
                load_whole(k, k)
            with sp.Fori(0, NE // 2 - 1) as k2:
                for slot in range(2):
                    sp.wait_ge(w_split, k2 * 2 + (slot + 1))
                    load_whole(k2 * 2 + (slot + 2), slot)
                    store_split(k2 * 2 + slot, slot)
            for slot in range(2):
                store_split(NE - 2 + slot, slot)
            for slot in range(2):
                sp.wait_ge(wr_stored[slot], NE // 2 * 16 + 16 * INIT)

            def store_part(c2, u, m):
                if m < PARTS - 1:
                    sp.wait_ge(part_ready[u], c2 * (PARTS - 1) + (m + 1) + INIT)
                else:
                    sp.wait_ge(last_ready[u], c2 + 1 + INIT)
                rows = DS[bass.ds(c2 * (2 * CW) + u * CW, CW), m * 2 * D:(m + 1) * 2 * D]
                sp.dma_start(rows.rearrange("(j p) f -> p j f", p=P), tiles(PB[u][:, m * 2 * CW:(m + 1) * 2 * CW], 2 * D)
                             ).then_inc(ds_stored[u][m], 16)

            store_part(0, 0, 0)
            with sp.Fori(0, NC // 2 - 1) as c2:
                for u in range(2):
                    store_part(c2 + u, 1 - u, 0)
                    for m in range(1, PARTS):
                        store_part(c2, u, m)
            store_part(NC // 2 - 1, 1, 0)
            for u in range(2):
                for m in range(1, PARTS):
                    store_part(NC // 2 - 1, u, m)
            sp.wait_ge(zero_rows, 16 * PARTS)

            def load_rows(tile, slot):
                rows = DS[bass.ds(tile * P + slot * (P // 2), P // 2), :]
                sp.dma_start(R[slot][:, :].rearrange("r (x f) -> r x f", f=2 * D),
                             rows.rearrange("(x b) (m f) -> (b m) x f", b=HB, m=PARTS)).then_inc(r_loaded[slot], 16)

            def load_expert(dst, src, k, loaded):
                sp.dma_start(dst[:, :], src[bass.ds(k, 1)].rearrange("a p f -> (a p) f")).then_inc(loaded, 16)

            def load_first(k, slot):
                sp.dma_start(W1S[slot][:, :], WR[bass.ds(k * P, P), :]).then_inc(w1_loaded[slot], 16)
                sp.dma_start(W1B[slot][:, :], w1[bass.ds(k, 1), :, 2 * H:2 * H + 2 * MH].rearrange("a p f -> (a p) f")
                             ).then_inc(w1_loaded[slot], 16)

            def load_gate(k, slot):
                sp.dma_start(GS[slot][:, :], GD[bass.ds(k, 1), :].broadcast_to([P, CW])
                             ).then_inc(g_loaded[slot], 16)

            for stored_part in ds_stored[0]:
                sp.wait_ge(stored_part, NC // 2 * 16 + 16 * INIT)
            load_rows(0, 0)
            load_rows(0, 1)
            for stored_part in ds_stored[1]:
                sp.wait_ge(stored_part, NC // 2 * 16 + 16 * INIT)
            sp.wait_ge(const_ready, 1)
            sp.dma_start(GD[0:SHARED, :], half_gate).then_inc(gd_stored, 16)

            def stage(s, scan, ffn):
                q = s - 1
                with sp.Fori(0, BODIES) as i:
                    for j in range(PER):
                        if ffn:
                            k = i * PER + j + SHARED
                            kk = q * NE + k
                            slot = j % 2
                            sp.wait_ge(m0_ready, (kk - 1) * MH + INIT)
                            load_first(k, slot)
                            sp.wait_ge(wg_ready, kk - 2 + INIT)
                            sp.wait_ge(wg1_ready, kk - 2 + INIT)
                            if j:
                                sp.wait_ge(gd_stored, s * 16 + 16)
                            load_gate(k - 1, 1 - slot)
                            sp.wait_ge(w2_done, kk - 2 + INIT)
                            load_expert(W2S[1 - slot], w2, k - 1, w2_loaded[1 - slot])
                        if scan and j % 2:
                            g = s * (TC // GT) + i * 2 + j // 2
                            sp.wait_ge(u_bc, g * (GT // 2) + GT // 2)
                            sp.wait_ge(dt_bc, g * (GT // 2) + GT // 2)
                            load_rows(s * CT + i + 1, j // 2)
                if ffn:
                    sp.wait_ge(wg_ready, s * NE - 2 + INIT)
                    sp.wait_ge(wg1_ready, s * NE - 2 + INIT)
                    load_gate(NE - 1, 1)
                    sp.wait_ge(w2_done, s * NE - 2 + INIT)
                    load_expert(W2S[1], w2, NE - 1, w2_loaded[1])
                if scan:
                    for k in range(SHARED):
                        if ffn:
                            sp.wait_ge(m0_ready, (s * NE + (k - 1)) * MH + INIT)
                        load_first(k, k)
                    if ffn:
                        sp.wait_ge(wg_ready, s * NE - 1 + INIT)
                        sp.wait_ge(wg1_ready, s * NE - 1 + INIT)
                    else:
                        sp.wait_ge(gd_stored, 16)
                    load_gate(0, 0)
                    if ffn:
                        sp.wait_ge(w2_done, s * NE - 1 + INIT)
                    load_expert(W2S[0], w2, 0, w2_loaded[0])
                if ffn:
                    sp.wait_ge(out_ready, s)
                    sp.dma_start(out[:, bass.ds(q * CW, CW)], O[:, :]).then_inc(stored, 16)

            stage(0, True, False)
            with sp.Fori(1, NC) as s:
                stage(s, True, True)
            stage(NC, False, True)
            sp.wait_ge(stored, 16 * NC + 16 * INIT)
            for r in r_loaded:
                sp.wait_ge(r, (1 + NC * BODIES) * 16)

        @block.gpsimd
        def _(pool):
            for started in (hr_done, hh_ready, wg_ready):
                pool.sem_inc(started, INIT)
            nc.gpsimd.memset(S[0][:, :], 0.0).then_inc(pool_const, 1)
            nc.gpsimd.memset(XC[:, :], 0.0).then_inc(pool_const, 1)
            nc.gpsimd.memset(mexp[:, :], -0.5).then_inc(pool_const, 1)
            pool.wait_ge(pool_const, 3)

            def inv_std(n):
                pool.wait_ge(var_ready, n + 1)
                nc.gpsimd.tensor_tensor(rstd[:, :], vareps[:, :], mexp[:, :], ALU.pow).then_inc(rstd_ready, 1)

            def low_weights(k2):
                for slot in range(2):
                    pool.wait_ge(w_high, k2 * 2 + (slot + 1))
                    nc.gpsimd.tensor_tensor(W1S[slot][:, 2 * H:4 * H].bitcast(F32R), WIN[slot],
                                            W1S[slot][:, 0:2 * H], ALU.subtract).then_inc(w_split, 1)

            with pool.Fori(0, NC // 2) as c2:
                for u in range(2):
                    c = c2 * 2 + u
                    inv_std(c)
                    low_weights(c)
                    pool.wait_ge(h_ready, c + 1)
                    cols = bass.ds(c2 * (2 * CW) + u * CW, CW)
                    nc.gpsimd.tensor_tensor(tiles(HR[:, cols]), tiles(Hn[u][:, :]), over_tiles(cst("outb")),
                                            ALU.add).then_inc(hr_done, 1)
                    nc.gpsimd.tensor_tensor(tiles(X[:, cols]), tiles(X[:, cols]), over_tiles(gbias[:, :]),
                                            ALU.add).then_inc(xg_done, 1)

            low_weights(NC)

            with pool.Fori(0, NC // 2) as c2:
                for u in range(2):
                    c = c2 * 2 + u
                    pool.wait_ge(part_ready[u], c2 * (PARTS - 1) + 1 + INIT)
                    pool.wait_ge(last_ready[u], c2 + INIT)
                    nc.gpsimd.tensor_tensor(REST[u][:, :], DU[u][:, :], PB[u][:, 0:2 * CW], ALU.subtract
                                            ).then_inc(rest_ready, 1)

            pool.wait_ge(du_ready, NC)
            nc.gpsimd.memset(CBLK[:, :], 0.0).then_inc(c_zero, 1)

            def dt_times_a(p, slot):
                pool.wait_ge(dtc_ready, p + 1)
                nc.gpsimd.tensor_tensor(tiles(dta[slot][:, :]), tiles(dtc[slot][:, :]), over_tiles(arep[:, :]),
                                        ALU.mult).then_inc(dta_ready, 1)

            def gated(kk, slot, gp):
                pool.wait_ge(th1_ready, kk + 1 + INIT)
                pool.wait_ge(hh_ready, kk + INIT)
                nc.gpsimd.tensor_tensor(tiles(wg_[:, :], CW)[:, :, 0:gp], tiles(th1[slot][:, :], CW)[:, :, 0:gp],
                                        GS[slot][:, 0:gp].unsqueeze(1).broadcast_to([P, MH, gp]), ALU.mult
                                        ).then_inc(wg_ready, 1)

            def hidden(kk, slot):
                pool.wait_ge(m0_ready, (kk + 1) * MH + INIT)
                pool.wait_ge(wg_ready, kk + 1 + INIT)
                pool.wait_ge(wg1_ready, kk + 1 + INIT)
                pool.wait_ge(w2_done, kk - 1 + INIT)
                nc.gpsimd.tensor_tensor(hh[slot][:, :], m0[slot][:, :], wg_[:, :], ALU.mult
                                        ).then_inc(hh_ready, 1)

            pool.wait_ge(arep_ready, 1)
            dt_times_a(0, 0)
            dt_times_a(1, 1)

            def stage(s, scan, ffn):
                q = s - 1

                def expert(kk, n, slot, prev, p):
                    if prev:
                        pool.wait_ge(g_loaded[1 - slot], n * 16)
                        gated(kk - 1, 1 - slot, GP if scan else GP_LAST)
                    if p is not None:
                        pool.wait_ge(a_ready, p + 1)
                        dt_times_a(p + 2, 0)
                    if prev:
                        hidden(kk - 1, 1 - slot)
                    if p is not None:
                        pool.wait_ge(a_ready, p + 2)
                        dt_times_a(p + 3, 1)

                with pool.Fori(0, BODIES) as i:
                    for j in range(PER):
                        p = s * (TC // 2) + i * PAIRS + 2 * j
                        kk = q * NE + i * PER + (j + SHARED)
                        n = q * (NE // 2) + i * 2 + (1 + (j + 1) // 2)
                        expert(kk, n, j % 2, ffn, p if scan else None)
                if ffn:
                    expert(s * NE, s * (NE // 2), 0, True, None)
                if scan:
                    inv_std(s * 2 + NC)
                    inv_std(s * 2 + (NC + 1))
                    expert(s * NE + 1, s * (NE // 2) + 1, 1, True, None)

            stage(0, True, False)
            with pool.Fori(1, NC) as s:
                stage(s, True, True)
            stage(NC, False, True)

        @block.tensor
        def _(pe):
            for started in (hT_ps, xt_ps, w2_done):
                pe.sem_inc(started, INIT)
            pe.sem_inc(y_done, SR)
            pe.wait_ge(ld_w, 48)
            pe.wait_ge(sct_ready, 1)
            nc.tensor.matmul(HA[:, 0:3 * D], sct[:, :], wmod_sb[:, 0:3 * D], start=True, stop=True)
            nc.tensor.matmul(HBk[:, 0:3 * D], sct[:, :], wmod_sb[:, 3 * D:6 * D], start=True, stop=True
                             ).then_inc(mod_ps, 1)
            pe.wait_ge(mod_ready, 1)
            ident = cst("ident")

            with pe.Fori(0, NC // 2) as c2:
                for u in range(2):
                    c = c2 * 2 + u
                    pe.wait_ge(h_ready, c + 1)
                    pe.wait_ge(hT_ready, c + INIT)
                    for j in range(CT):
                        mm = nc.tensor.transpose(HA[:, j * D:(j + 1) * D], Hn[u][:, j * D:(j + 1) * D], ident)
                    mm.then_inc(hT_ps, 1)
                    pe.wait_ge(hT_ready, c + 1 + INIT)
                    pe.wait_ge(z_ready, c + INIT)
                    nc.tensor.matmul(HBk[:, :], cst("win")[:, 0:D], hT[u][:, :], start=True, stop=True
                                     ).then_inc(inp_ps, 1)
                    nc.tensor.matmul(HC[:, :], cst("win")[:, D:2 * D], hT[u][:, :], start=True, stop=True
                                     ).then_inc(inp_ps, 1)

            with pe.Fori(0, NC // 2) as c2:
                for u in range(2):
                    c = c2 * 2 + u
                    pe.wait_ge(xst_ready, c + 1)
                    pe.wait_ge(dti_ready, c + INIT)
                    for j in range(CT):
                        mm = nc.tensor.matmul(U0[:, j * D:(j + 1) * D], hT[u][:, j * D:(j + 1) * D], cst("wdt"),
                                              start=True, stop=True)
                    mm.then_inc(dt_ps, 1)
                    pe.wait_ge(xtok_ready, c + INIT)
                    for j in range(CT):
                        mm = nc.tensor.transpose(U1[:, j * D:(j + 1) * D], hT[u][:, j * D:(j + 1) * D], ident)
                    mm.then_inc(xt_ps, 1)

            pe.wait_ge(xs_ready, NC)
            pe.wait_ge(z_ready, NC + INIT)
            xs3 = XS[:, :].rearrange("p (t b) -> p t b", b=B)
            for w, banks in (("wb", (HA, HBk)), ("wc", (HC, YSC))):
                for b in range(B):
                    mm = nc.tensor.matmul(banks[b // HB][N * (b % HB):N * (b % HB) + N, :], cst(w),
                                          xs3[:, :, b], start=True, stop=True)
            mm.then_inc(bc_ps, 1)

            def spread(bnk, n, what, ready):
                w = 4 * SW
                rows = R[n // 4 % 2][:, n % 4 * w:(n % 4 + 1) * w].rearrange("p (t q d) -> p t q d", q=2, d=D)
                nc.tensor.matmul(tiles(bnk[:, :]), spread_bf[:, :], rows[:, :, what, :], start=True, stop=True
                                 ).then_inc(ready, 1)

            pe.wait_ge(dti_ready, NC + INIT)
            pe.wait_ge(xtok_ready, NC + INIT)
            pe.wait_ge(r_loaded[0], 16)
            spread(U[0], 0, 1, u_bc)
            spread(DTB, 0, 0, dt_bc)
            pe.wait_ge(dtc_ready, 1)
            spread(DTB, 1, 0, dt_bc)
            pe.wait_ge(c_ready, 2)

            def stage(s, scan, ffn):
                q = s - 1

                def readout(i, n):
                    for h in range(2):
                        tl = i * (2 * PAIRS) + (2 * n + h)
                        pe.wait_ge(s_done, (s * TC + tl + 1) * 2 + INIT)
                        for half in range(2):
                            mm = nc.tensor.matmul(
                                YSC[:, bass.ds(tl * B + half * HB, HB)],
                                S[(2 * n + h) % SR][:, half * D:(half + 1) * D],
                                CBLK[:, bass.ds((s * TC + tl) * B + half * HB, HB)], start=True, stop=True)
                        mm.then_inc(y_done, 1)

                def pair(i, n):
                    p = s * (TC // 2) + i * PAIRS + n
                    body = s * BODIES + i
                    if n:
                        readout(i, n - 1)
                    if (n + 1) % 4 == 0:
                        pe.wait_ge(r_loaded[(n + 1) // 4 % 2], (body + 1 + (n + 1) // 8) * 16)
                    pe.wait_ge(q_done, p * 4 + INIT)
                    spread(U[(n + 1) % 2], n + 1, 1, u_bc)
                    if (n + 2) % 4 == 0:
                        pe.wait_ge(r_loaded[(n + 2) // 4 % 2], (body + 1 + (n + 2) // 8) * 16)
                    pe.wait_ge(dtc_ready, p + 2)
                    if ffn and n == 0:
                        pe.wait_ge(gT_ready, s)
                    spread(DTB, n + 2, 0, dt_bc)

                def second(kk, n, slot, m, last=False):
                    if m == 0:
                        pe.wait_ge(hh_ready, kk + 1 + INIT)
                        pe.wait_ge(w2_loaded[slot], n * 16)
                    mm = nc.tensor.matmul(YACC[:, :], W2S[slot][:, m * D:(m + 1) * D],
                                          hh[slot][:, m * CW:(m + 1) * CW],
                                          start=False, stop=last, skip_group_check=True)
                    if m == MH - 1:
                        mm.then_inc(w2_done, 1)

                def first(bnk, slot, c):
                    for a, b in ((0, 0), (0, 1), (1, 0)):
                        mm = nc.tensor.matmul(bnk[:, :], W1S[slot][:, a * 2 * H + c:a * 2 * H + c + D].bitcast(F32R),
                                              XR[:, b * CW:(b + 1) * CW].bitcast(F32R),
                                              start=(a + b == 0), stop=(a == 1))
                    return mm

                def expert(kk, n, slot, prev, i, pr):
                    for m in range(MH):
                        if kk is not None:
                            if m == 0:
                                pe.wait_ge(w1_loaded[slot], n * 32)
                            pe.wait_ge(hb_ready, kk * MH + m + INIT)
                            first(HA, slot, m * D).then_inc(h1_ps, 1)
                            if m == 0:
                                pe.wait_ge(m0_ready, kk * MH + INIT)
                            first((HBk, HC)[m], slot, H + m * D).then_inc(h11_ps, 1)
                        if pr is not None:
                            pair(i, pr + m)
                        if prev:
                            second(kk - 2, n - 1, slot, m)

                with pe.Fori(0, BODIES) as i:
                    for j in range(PER):
                        expert(q * NE + i * PER + (j + SHARED) if ffn else None,
                               q * (NE // 2) + i * 2 + (2 + j // 2), j % 2, ffn, i, 2 * j if scan else None)
                    if scan:
                        readout(i, PAIRS - 1)
                if scan:
                    pe.wait_ge(yg_ready, s + 1)
                    if ffn:
                        pe.wait_ge(hb_ready, s * NE * MH + INIT)
                    for j in range(CT):
                        mm = nc.tensor.matmul(HA[:, j * D:(j + 1) * D], ygT[:, j * D:(j + 1) * D], cst("wout"),
                                              start=True, stop=True)
                    mm.then_inc(o_ps, 1)
                if ffn:
                    nc.tensor.matmul(YACC[:, :], b2_sb[:, :], gT[:, :], start=False, stop=False,
                                     skip_group_check=True)
                    for slot in range(2):
                        for m in range(MH):
                            second(s * NE - 2 + slot, s * (NE // 2), slot, m, slot == 1 and m == MH - 1)
                    pe.wait_ge(yT_ready, s)
                    if scan:
                        pe.wait_ge(q_done, (s + 1) * TC * 2 + INIT)
                    for j in range(CT):
                        mm = nc.tensor.transpose(U1[:, j * D:(j + 1) * D], yT[:, j * D:(j + 1) * D], ident)
                    mm.then_inc(yt_ps, 1)
                if scan:
                    nc.tensor.matmul(YACC[:, :], cst("bs2")[32:34, :], half_gate, start=True, stop=False,
                                     skip_group_check=True)
                    pe.wait_ge(h2_ready, s + 1)
                    for j in range(CT):
                        mm = nc.tensor.transpose(HBk[:, j * D:(j + 1) * D], Hn[0][:, j * D:(j + 1) * D], ident)
                    mm.then_inc(h2T_ps, 1)
                    pe.wait_ge(h2T_ready, s + 1)
                    pe.wait_ge(dtc_ready, (s + 1) * (TC // 2) + 2)
                    for j in range(CT):
                        mm = nc.tensor.matmul(DTB[:, j * E:(j + 1) * E], h2T[:, j * D:(j + 1) * D], cst("wg"),
                                              start=True, stop=True)
                    mm.then_inc(lg_ps, 1)
                    pe.wait_ge(xr_ready, s + 1)
                    for k in range(SHARED):
                        expert(s * NE + k, s * (NE // 2) + 1, k, False, 0, None)
                    pe.wait_ge(gt_ready, s + 1)
                    for j in range(CT):
                        mm = nc.tensor.transpose(DTB[0:E, j * D:(j + 1) * D], gt[:, j * E:(j + 1) * E], ident)
                    mm.then_inc(gT_ps, 1)

            stage(0, True, False)
            with pe.Fori(1, NC) as s:
                stage(s, True, True)
            stage(NC, False, True)

        @block.scalar
        def _(act):
            for started in (hT_ready, z_ready, hb_ready, th1_ready, dte_ready, *part_ready):
                act.sem_inc(started, INIT)
            act.wait_ge(ld_w, 48)
            nc.scalar.activation(sct[:, :], cst("ct"), ACT.Silu).then_inc(sct_ready, 1)

            def silu(c):
                act.wait_ge(conv_done, c + 1)
                nc.scalar.activation(XS[:, bass.ds(c * CW, CW)], XS[:, bass.ds(c * CW, CW)], ACT.Silu
                                     ).then_inc(xs_ready, 1)

            def project(c, u, conv):
                act.wait_ge(hT_ps, c + 1 + INIT)
                nc.scalar.copy(hT[u][:, :], HA[:, :]).then_inc(hT_ready, 1)
                if conv:
                    silu(c - LAG)
                act.wait_ge(inp_ps, c * 2 + 1)
                nc.scalar.activation(XC[:, bass.ds(c * CW + XPAD * B, CW)], HBk[:, :], ACT.Identity,
                                     bias=col(IN_B)).then_inc(xc_ready, 1)
                act.wait_ge(inp_ps, c * 2 + 2)
                nc.scalar.activation(ZG[:, bass.ds(c * CW, CW)], HC[:, :], ACT.Silu,
                                     bias=col(IN_B + 1)).then_inc(z_ready, 1)

            def high_weights(k2):
                for slot in range(2):
                    act.wait_ge(w_loaded[slot], k2 * 16 + 16)
                    act.wait_ge(wr_stored[slot], k2 * 16 + 16 * INIT)
                    nc.scalar.copy(W1S[slot][:, 0:2 * H].bitcast(F32R), WIN[slot]).then_inc(w_high, 1)

            act.wait_ge(pool_const, 2)
            for c in range(4):
                high_weights(c)
                project(c, c % 2, c >= LAG)
            with act.Fori(2, NC // 2) as c2:
                for u in range(2):
                    high_weights(c2 * 2 + u)
                    project(c2 * 2 + u, u, True)
            high_weights(NC)
            for c in range(NC - LAG, NC):
                silu(c)

            act.wait_ge(const_ready, 1)
            nc.scalar.activation(arep[:, :], arep[:, :], ACT.Exp).then_inc(aexp_ready, 1)
            act.wait_ge(xs_ready, NC)
            def copy_xs(c, u):
                act.wait_ge(xt_ps, c - 1 + INIT)
                nc.scalar.copy(hT[u][:, :], XS[:, bass.ds(c * CW, CW)]).then_inc(xst_ready, 1)

            def exp_dt(c):
                act.wait_ge(dti_ready, c + 1 + INIT)
                nc.scalar.activation(XC[:, bass.ds(c * CW, CW)], XC[:, bass.ds(c * CW, CW)], ACT.Exp
                                     ).then_inc(dte_ready, 1)

            copy_xs(0, 0)
            with act.Fori(0, NC // 2 - 1) as c2:
                for u in range(2):
                    copy_xs(c2 * 2 + u + 1, 1 - u)
                    exp_dt(c2 * 2 + u)
            copy_xs(NC - 1, 1)
            for c in range(NC - 2, NC):
                exp_dt(c)
            act.wait_ge(dte_ready, NC + INIT)
            for h in range(4):
                v = XC[:, h * 2 * CW:(h + 1) * 2 * CW]
                nc.scalar.activation(v, v, ACT.Ln, bias=col(ONE)).then_inc(dtl_ready, 1)

            act.wait_ge(bc_ps, 1)
            for half, bnk in enumerate((HA, HBk)):
                last = nc.scalar.activation(BCOL[:, half * (T + GT):half * (T + GT) + T], bnk[:, :], ACT.Identity,
                                            bias=col(B_B))
            last.then_inc(bcol_ready, 1)

            def part(m, c2, u, src):
                act.wait_ge(ds_stored[u][m], c2 * 16 + 16 * INIT)
                nc.scalar.copy(PB[u][:, m * 2 * CW:(m + 1) * 2 * CW], src[:, :]).then_inc(part_ready[u], 1)

            def lead(c, c2, u):
                act.wait_ge(du_ready, c + 1)
                part(0, c2, u, DU[u])

            def middle(c, c2, u):
                act.wait_ge(rest_ready, c + 1)
                part(1, c2, u, REST[u])

            act.wait_ge(w_split, NE)
            lead(0, 0, 0)
            with act.Fori(0, NC // 2 - 1) as c2:
                lead(c2 * 2 + 1, c2, 1)
                middle(c2 * 2, c2, 0)
                lead(c2 * 2 + 2, c2 + 1, 0)
                middle(c2 * 2 + 1, c2, 1)
            lead(NC - 1, NC // 2 - 1, 1)
            middle(NC - 2, NC // 2 - 1, 0)
            middle(NC - 1, NC // 2 - 1, 1)

            def copy_dt(p, slot):
                act.wait_ge(dt_bc, p + 1)
                nc.scalar.copy(dtc[slot][:, :], DTB[:, :]).then_inc(dtc_ready, 1)

            def exp_dta(p, slot):
                act.wait_ge(dta_ready, p + 1)
                nc.scalar.activation(ab[slot][:, :], dta[slot][:, :], ACT.Exp).then_inc(a_ready, 1)

            copy_dt(0, 0)
            copy_dt(1, 1)

            act.wait_ge(c_zero, 1)
            cv = CBLK[:, :].rearrange("p (t h b) -> p t h b", h=2, b=HB)

            def c_blocks(half, bnk):
                for b in range(HB):
                    r = slice(N * b, N * b + N)
                    last = nc.scalar.activation(cv[r, :, half, b], bnk[r, :], ACT.Identity,
                                                bias=wc_sb[r, c0 + C_B:c0 + C_B + 1])
                last.then_inc(c_ready, 1)

            c_blocks(1, YSC)
            exp_dta(0, 0)
            c_blocks(0, HC)

            def stage(s, scan, ffn):
                q = s - 1

                def copy_ahead(i, n):
                    p = s * (TC // 2) + i * PAIRS + n
                    act.wait_ge(dta_ready, p + 1)
                    copy_dt(p + 2, n % 2)

                def exp_ahead(i, n):
                    p = s * (TC // 2) + i * PAIRS + n
                    act.wait_ge(p_done, p * 4 + INIT)
                    exp_dta(p + 1, (n + 1) % 2)

                def pre(kk, slot, m):
                    act.wait_ge(h1_ps, kk * MH + (m + 1))
                    nc.scalar.activation(hb[slot][:, m * CW:(m + 1) * CW], HA[:, :], ACT.Identity,
                                         bias=W1B[slot][:, m:m + 1]).then_inc(hb_ready, 1)

                def tanh(kk, slot):
                    act.wait_ge(hb_ready, kk * MH + MH + INIT)
                    act.wait_ge(th1_ready, kk + INIT)
                    act.wait_ge(wg1_ready, kk + INIT)
                    nc.scalar.activation(th[:, :], hb[slot][:, :], ACT.Tanh, scale=0.5).then_inc(th_ready, 1)

                def one_plus(kk, slot):
                    act.wait_ge(th_ready, kk + 1)
                    act.wait_ge(wg_ready, kk - 1 + INIT)
                    gp = GP if scan else GP_LAST
                    nc.scalar.activation(tiles(th1[slot][:, :], CW)[:, :, 0:gp], tiles(th[:, :], CW)[:, :, 0:gp], ACT.Identity, bias=col(ONE)
                                         ).then_inc(th1_ready, 1)

                with act.Fori(0, BODIES) as i:
                    for j in range(PER):
                        kk, slot = q * NE + i * PER + (j + SHARED), j % 2
                        for m in range(MH):
                            if ffn:
                                pre(kk, slot, m)
                            if scan:
                                exp_ahead(i, 2 * j + m)
                            if ffn and m:
                                tanh(kk, slot)
                            if scan:
                                copy_ahead(i, 2 * j + m)
                        if ffn:
                            one_plus(kk, slot)
                if ffn:
                    act.wait_ge(w2_done, s * NE + INIT)
                    nc.scalar.copy(yT[:, :], YACC[:, :]).then_inc(yT_ready, 1)
                if scan:
                    act.wait_ge(h2T_ps, s + 1)
                    nc.scalar.copy(h2T[:, :], HBk[:, :]).then_inc(h2T_ready, 1)
                    nc.scalar.copy(XR[:, 0:CW].bitcast(F32R), HBk[:, :]).then_inc(xh_ready, 1)
                    k0, k1 = s * NE, s * NE + 1
                    pre(k0, 0, 0)
                    act.wait_ge(lgd_ready, s + 1)
                    nc.scalar.activation(ex[:, :], rp[:, :], ACT.Exp).then_inc(ex_ready, 1)
                    pre(k0, 0, 1)
                    tanh(k0, 0)
                    pre(k1, 1, 0)
                    one_plus(k0, 0)
                    pre(k1, 1, 1)
                    tanh(k1, 1)
                    one_plus(k1, 1)
                    act.wait_ge(gT_ps, s + 1)
                    nc.scalar.copy(gT[:, :], DTB[0:E, :]).then_inc(gT_ready, 1)
                    act.wait_ge(gT_ready, s + 1)
                    act.dma_start(GD[SHARED:NE, :], gT[:, :]).then_inc(gd_stored, 16)
                    if ffn:
                        act.wait_ge(out_ready, s)
                    act.wait_ge(x2_ready, s + 1)
                    nc.scalar.copy(X2[:, :], X2n[:, :]).then_inc(x2_kept, 1)

            stage(0, True, False)
            with act.Fori(1, NC) as s:
                stage(s, True, True)
            stage(NC, False, True)

        @block.vector
        def _(dve):
            for started in (dti_ready, xtok_ready, *last_ready, s_done, p_done, q_done, m0_ready, wg1_ready):
                dve.sem_inc(started, INIT)
            own = Chain(dve, dve_own)
            V = nc.vector
            dve.wait_ge(ld_w, 48)
            own(V.tensor_copy(spread_bf[:, :], cst("sel")[0:ROWS, :]))
            own(V.memset(S[SR - 1][:, :], 0.0))
            own(V.memset(half_gate, 0.5))
            own(V.tensor_scalar(arep[:, :], cst("arep"), -5.0, 2.0, ALU.max, ALU.min))
            own(V.tensor_scalar(b2_sb[:, :], b2_sb[:, :], 2.0, None, ALU.mult))
            own.wait()
            nc.vector.engine_nop().then_inc(const_ready, 1)
            dve.wait_ge(mod_ps, 1)
            own(V.tensor_copy(mods[:, 0:3 * D], HA[:, 0:3 * D]))
            own(V.tensor_copy(mods[:, 3 * D:6 * D], HBk[:, 0:3 * D]))
            own.wait()
            for m in (CA, CB):
                own(V.tensor_scalar(m, m, 1.0, None, ALU.add))
            for i, g in enumerate((GA, GB)):
                own(V.scalar_tensor_tensor(out=gmag[:, i * D:(i + 1) * D], in0=g, scalar=-1.0, in1=g,
                                           op0=ALU.mult, op1=ALU.max))
                own(V.tensor_scalar(gsgn[:, i * D:(i + 1) * D], g, 0.0, 2.0, ALU.is_ge, ALU.mult))
            own.wait()
            own(V.tensor_scalar(gmag[:, :], gmag[:, :], 0.25, None, ALU.max))
            own.wait()
            for i, g in enumerate((GA, GB)):
                own(V.scalar_tensor_tensor(out=g, in0=gsgn[:, i * D:(i + 1) * D], scalar=-1.0,
                                           in1=gmag[:, i * D:(i + 1) * D], op0=ALU.add, op1=ALU.mult))
            own.wait()
            own(V.tensor_tensor(gg[:, :], GA, cst("lng"), ALU.mult))
            own(V.tensor_tensor(gbias[:, :], GA, cst("lnb"), ALU.mult))
            own.wait()
            V.engine_nop().then_inc(mod_ready, 1)

            def normalise(dst, src, n, scale, out, add, done, fill=None):
                for j in range(CT):
                    own(V.bn_stats(st[:, 6 * j:6 * j + 6], src(j)))
                own.wait()
                s3 = st[:, :].rearrange("p (j k) -> p j k", k=6)
                own(V.tensor_tensor(mean[:, :], s3[:, :, 1], s3[:, :, 4], ALU.add))
                own(V.tensor_tensor(mdif[:, :], s3[:, :, 1], s3[:, :, 4], ALU.subtract))
                own(V.tensor_tensor(vsum[:, :], s3[:, :, 2], s3[:, :, 5], ALU.add))
                own.wait()
                own(V.tensor_scalar(mean[:, :], mean[:, :], 0.5, None, ALU.mult))
                own(V.tensor_tensor(mdif[:, :], mdif[:, :], mdif[:, :], ALU.mult))
                own(V.tensor_scalar(vsum[:, :], vsum[:, :], 1.0 / D, EPS, ALU.mult, ALU.add))
                own.wait()
                V.scalar_tensor_tensor(out=vareps[:, :], in0=mdif[:, :], scalar=0.25, in1=vsum[:, :],
                                       op0=ALU.mult, op1=ALU.add).then_inc(var_ready, 1)
                for j in range(CT):
                    own(V.scalar_tensor_tensor(out=dst[:, j * D:(j + 1) * D], in0=src(j), scalar=mean[:, j:j + 1],
                                               in1=scale, op0=ALU.subtract, op1=ALU.mult))
                    if fill:
                        own.wait(1)
                        fill(j)
                own.wait()
                dve.wait_ge(rstd_ready, n + 1)
                for j in range(CT):
                    last = V.scalar_tensor_tensor(out=out(j), in0=dst[:, j * D:(j + 1) * D], scalar=rstd[:, j:j + 1],
                                                  in1=add(j), op0=ALU.mult, op1=ALU.add)
                    if j < CT - 1:
                        own(last)
                last.then_inc(done, 1)

            def by_feature(dst, a, b, op):
                return V.tensor_tensor(tiles(dst), tiles(a), over_tiles(b), op)

            def tap(c, k):
                return XC[:, bass.ds(c * CW + k * B, CW)]

            def convolve(c, k):
                y = XS[:, bass.ds(c * CW, CW)]
                if k == 0:
                    own(V.tensor_scalar(y, tap(c, 0), col(CONV_W), col(CONV_B), ALU.mult, ALU.add))
                    return
                ins = V.scalar_tensor_tensor(out=y, in0=tap(c, k), scalar=col(CONV_W + k), in1=y,
                                             op0=ALU.mult, op1=ALU.add)
                if k < KW - 1:
                    own(ins)
                else:
                    ins.then_inc(conv_done, 1)

            def modulate(c, u, conv):
                dve.wait_ge(hT_ps, c - 1 + INIT)
                dve.wait_ge(hr_done, c - 1 + INIT)

                def fill(k):
                    if k == 0:
                        dve.wait_ge(xc_ready, c - LAG + 2)
                    convolve(c - LAG, k)

                normalise(Hn[u], lambda j: X[:, bass.ds(c * CW + j * D, D)], c, CA,
                          lambda j: Hn[u][:, j * D:(j + 1) * D], lambda j: SA, h_ready,
                          fill if conv else None)

            dve.wait_ge(ld_x, 16)
            for c in range(4):
                modulate(c, c % 2, c >= LAG)
            own.at(own.base + own.n)
            start, per = own.base, 2 * (3 * CT + 5 + KW - 1)
            with dve.Fori(2, NC // 2) as c2:
                own.at((c2 - 2) * per + start)
                for u in range(2):
                    modulate(c2 * 2 + u, u, True)
                assert own.n == per
            own.at(start + (NC // 2 - 2) * per)
            for c in range(NC - LAG, NC):
                dve.wait_ge(xc_ready, min(c + 2, NC))
                for k in range(KW):
                    own.wait()
                    convolve(c, k)

            with dve.Fori(0, NC // 2) as c2:
                for u in range(2):
                    c = c2 * 2 + u
                    dve.wait_ge(dt_ps, c + 1)
                    by_feature(XC[:, bass.ds(c * CW, CW)], U0[:, :], cst("dtb"), ALU.add).then_inc(dti_ready, 1)
                    dve.wait_ge(xt_ps, c + 1 + INIT)
                    V.tensor_copy(XTOK[:, bass.ds(c * CW, CW)], U1[:, :]).then_inc(xtok_ready, 1)
            dve.wait_ge(xtok_ready, NC + INIT)

            def dt_and_u(c, u):
                du = DU[u][:, :].rearrange("p (j q d) -> p j q d", q=2, d=D)
                V.tensor_scalar(du[:, :, 0, :], tiles(XC[:, bass.ds(c * CW, CW)]), 0.001, 0.2, ALU.max, ALU.min
                                ).then_inc(dt_clipped, 1)
                dve.wait_ge(dt_clipped, c + 1)
                V.tensor_tensor(du[:, :, 1, :], du[:, :, 0, :], tiles(XTOK[:, bass.ds(c * CW, CW)]), ALU.mult
                                ).then_inc(du_ready, 1)

            def last_part(c2, u):
                dve.wait_ge(part_ready[u], c2 * (PARTS - 1) + 2 + INIT)
                dve.wait_ge(ds_stored[u][2], c2 * 16 + 16 * INIT)
                V.tensor_tensor(PB[u][:, 4 * CW:6 * CW], REST[u][:, :], PB[u][:, 2 * CW:4 * CW], ALU.subtract
                                ).then_inc(last_ready[u], 1)

            dve.wait_ge(dtl_ready, 1)
            dt_and_u(0, 0)
            dt_and_u(1, 1)
            dve.wait_ge(dtl_ready, 4)
            with dve.Fori(0, NC // 2 - 1) as c2:
                for u in range(2):
                    dve.wait_ge(rest_ready, c2 * 2 + u + 1)
                    dt_and_u(c2 * 2 + u + 2, u)
                    last_part(c2, u)
            for u in range(2):
                last_part(NC // 2 - 1, u)
            dve.wait_ge(aexp_ready, 1)
            V.tensor_scalar(arep[:, :], arep[:, :], -1.0, None, ALU.mult).then_inc(arep_ready, 1)
            dve.wait_ge(bcol_ready, 1)
            b3 = BCOL[:, :].rearrange("p (h t) -> p h t", h=2)
            own(V.memset(b3[:, :, T:T + GT], 0.0))

            def group_scalars(g, slot):
                return V.tensor_copy(BNOW[slot][:, :].rearrange("p (h t) -> p h t", h=2),
                                     b3[:, :, bass.ds(g * GT, GT)])

            own.wait()
            own(group_scalars(0, 0))
            own.wait()
            per_stage = 6 * CT + 28

            def stage(s, scan, ffn):
                q = s - 1

                def step(i, n, h):
                    p = s * (TC // 2) + i * PAIRS + n
                    t = s * TC + i * (2 * PAIRS) + (2 * n + h)
                    now, prev = S[(2 * n + h) % SR], S[(2 * n + h - 1) % SR]
                    if h == 0:
                        dve.wait_ge(a_ready, p + 1)
                        dve.wait_ge(u_bc, p + 1)
                    halves = [slice(half * D, (half + 1) * D) for half in range(2)]
                    for half, r in enumerate(halves):
                        dve.wait_ge(s_done, t * 2 + half - 1 + INIT)
                        V.tensor_tensor(pt[:, r], prev[:, r], ab[n % 2][:, h * SW + half * D:h * SW + (half + 1) * D],
                                        ALU.mult).then_inc(p_done, 1)
                    if n % 4 == 2 and h == 0:
                        group_scalars(s * (TC // GT) + i * 2 + (n // 4 + 1), 1 - n // 4)
                    for half, r in enumerate(halves):
                        k = half * GT + 2 * n % GT + h
                        dve.wait_ge(p_done, t * 2 + half + 1 + INIT)
                        V.scalar_tensor_tensor(out=qt[:, r], in0=U[n % 2][:, h * SW + half * D:h * SW + (half + 1) * D],
                                               scalar=BNOW[n // 4][:, k:k + 1], in1=pt[:, r],
                                               op0=ALU.mult, op1=ALU.add).then_inc(q_done, 1)
                    for half, r in enumerate(halves):
                        dve.wait_ge(q_done, t * 2 + half + 1 + INIT)
                        V.tensor_scalar(now[:, r], qt[:, r], 10.0, -10.0, ALU.min, ALU.max).then_inc(s_done, 1)

                def gate(kk, slot, m):
                    dve.wait_ge(hb_ready, kk * MH + (m + 1) + INIT)
                    dve.wait_ge(h11_ps, kk * MH + (m + 1))
                    r = slice(m * CW, (m + 1) * CW)
                    V.scalar_tensor_tensor(out=m0[slot][:, r], in0=(HBk, HC)[m][:, :],
                                           scalar=W1B[slot][:, MH + m:MH + m + 1],
                                           in1=hb[slot][:, r], op0=ALU.add, op1=ALU.mult).then_inc(m0_ready, 1)

                def gated(kk, slot, n):
                    dve.wait_ge(g_loaded[slot], n * 16)
                    dve.wait_ge(th_ready, kk + 1)
                    dve.wait_ge(hh_ready, kk + INIT)
                    gp = GP if scan else GP_LAST
                    V.scalar_tensor_tensor(out=tiles(wg_[:, :], CW)[:, :, gp:CW], in0=tiles(th[:, :], CW)[:, :, gp:CW],
                                           scalar=1.0,
                                           in1=GS[slot][:, gp:CW].unsqueeze(1).broadcast_to([P, MH, CW - gp]),
                                           op0=ALU.add, op1=ALU.mult).then_inc(wg1_ready, 1)

                if ffn:
                    own.at(q * per_stage + before)
                with dve.Fori(0, BODIES) as i:
                    for j in range(PER):
                        kk = q * NE + i * PER + (j + SHARED)
                        if scan:
                            step(i, 2 * j, 0)
                        if ffn:
                            gated(kk - 1, 1 - j % 2, q * (NE // 2) + i * 2 + (1 + (j + 1) // 2))
                        if scan:
                            step(i, 2 * j, 1)
                        if ffn:
                            gate(kk, j % 2, 0)
                        if scan:
                            step(i, 2 * j + 1, 0)
                            step(i, 2 * j + 1, 1)
                        if ffn:
                            gate(kk, j % 2, 1)
                if ffn:
                    gated(s * NE - 1, 1, s * (NE // 2))
                if scan:
                    cols = bass.ds(s * CW, CW)
                    dve.wait_ge(y_done, (s + 1) * TC + SR)
                    V.tensor_tensor(ygT[:, :], YSC[:, :], ZG[:, cols], ALU.mult).then_inc(yg_ready, 1)
                    dve.wait_ge(o_ps, s + 1)
                    own(V.tensor_tensor(om[:, :], HA[:, :], HR[:, cols], ALU.add))
                    own.wait()
                    normalise(om, lambda j: om[:, j * D:(j + 1) * D], s * 2 + NC, gg[:, :],
                              lambda j: X2n[:, j * D:(j + 1) * D], lambda j: X[:, bass.ds(s * CW + j * D, D)], x2_ready)
                    dve.wait_ge(x2_ready, s + 1)
                    normalise(Hn[0], lambda j: X2n[:, j * D:(j + 1) * D], s * 2 + (NC + 1), CB,
                              lambda j: Hn[0][:, j * D:(j + 1) * D], lambda j: SB, h2_ready)
                if ffn:
                    dve.wait_ge(yt_ps, s)
                    dve.wait_ge(stored, q * 16 + 16 * INIT)
                    dve.wait_ge(x2_kept, s)
                    own(by_feature(O[:, :], U1[:, :], GB, ALU.mult))
                    own.wait()
                    V.tensor_tensor(O[:, :], O[:, :], X2[:, :], ALU.add).then_inc(out_ready, 1)
                if scan:

                    def e3(ap):
                        return ap.rearrange("p (j e) -> p j e", e=E)

                    def over_e(ap):
                        return ap.unsqueeze(2).broadcast_to([P, CT, E])

                    dve.wait_ge(xh_ready, s + 1)
                    dve.wait_ge(h2T_ready, s + 1)
                    V.tensor_tensor(XR[:, CW:2 * CW].bitcast(F32R), h2T[:, :], XR[:, 0:CW], ALU.subtract
                                    ).then_inc(xr_ready, 1)
                    order = cst("order").unsqueeze(1).broadcast_to([P, CT, E])
                    dve.wait_ge(lg_ps, s + 1)
                    own(V.tensor_copy(lg[:, :], DTB[:, 0:CT * E]))
                    own.wait()

                    def first_largest(top, src, pick):
                        own(V.tensor_reduce(top, e3(src), AX.X, ALU.max))
                        own.wait()
                        own(V.tensor_tensor(e3(pick), e3(src), over_e(top), ALU.is_equal))
                        own.wait()
                        own(V.tensor_tensor(e3(pick), e3(pick), order, ALU.mult))
                        own.wait()
                        own(V.tensor_reduce(place[:, :], e3(pick), AX.X, ALU.max))
                        own.wait()
                        own(V.tensor_tensor(e3(pick), e3(pick), over_e(place[:, :]), ALU.is_equal))
                        own.wait()

                    first_largest(top[:, :], lg[:, :], pick1[:, :])
                    V.tensor_tensor(e3(rp[:, :]), e3(lg[:, :]), over_e(top[:, :]), ALU.subtract
                                    ).then_inc(lgd_ready, 1)
                    own(V.scalar_tensor_tensor(out=lg[:, :], in0=pick1[:, :], scalar=-1e38, in1=lg[:, :],
                                               op0=ALU.mult, op1=ALU.add))
                    own.wait()
                    first_largest(top2[:, :], lg[:, :], pick2[:, :])
                    gate(s * NE, 0, 0)
                    own(V.tensor_tensor(pick1[:, :], pick1[:, :], pick2[:, :], ALU.add))
                    own.wait()
                    dve.wait_ge(ex_ready, s + 1)
                    own(V.tensor_tensor(ex[:, :], ex[:, :], pick1[:, :], ALU.mult))
                    own.wait()
                    own(V.tensor_reduce(gsum[:, :], e3(ex[:, :]), AX.X, ALU.add))
                    gate(s * NE, 0, 1)
                    own.wait()
                    own(V.reciprocal(grec[:, :], gsum[:, :]))
                    own.wait()
                    V.scalar_tensor_tensor(out=e3(gt[:, :]), in0=e3(ex[:, :]), scalar=0.5, in1=over_e(grec[:, :]),
                                           op0=ALU.mult, op1=ALU.mult).then_inc(gt_ready, 1)
                    dve.wait_ge(hh_ready, s * NE + INIT)
                    gate(s * NE + 1, 1, 0)
                    gated(s * NE, 0, s * (NE // 2) + 1)
                    gate(s * NE + 1, 1, 1)

            stage(0, True, False)
            before = own.base + own.n
            with dve.Fori(1, NC) as s:
                stage(s, True, True)
                assert own.n == per_stage, own.n
            stage(NC, False, True)


def kernel(**inputs):
    import numpy as np
    import concourse.bacc as bacc
    from concourse.bass_utils import run_bass_kernel_spmd

    g = {k: np.asarray(v) for k, v in inputs.items()}

    def a(name):
        return g["L0_attn_" + name]

    def f(name):
        return g["L0_ffn_" + name]

    def row(v):
        return np.broadcast_to(v[None, :], (P, v.shape[0]))

    def hidden_cols(v):
        return v.reshape(MH, P).T

    d = D
    sel = np.zeros((P, P), np.float32)
    for r in range(ROWS):
        sel[r, N * (r // PARTS):N * (r // PARTS) + N] = 1.0
    cols = np.zeros((P, 16), np.float32)
    cols[:, 0:2] = a("in_proj_b").reshape(2, d).T
    cols[:, 2:6] = a("conv_w")[:, 0, :]
    cols[:, 6] = a("conv_b")
    cols[:, 7] = np.tile(a("B_b"), HB)
    cols[:, 8] = np.tile(a("C_b"), HB)
    cols[:, 9] = 1.0
    wcol = np.concatenate([
        a("in_proj_w").T, a("dt_w").T, a("B_w").T, a("C_w").T, a("out_w").T, f("Wg"),
        np.tile(a("A_log").T, (HB, 1)), np.eye(P, dtype=np.float32), np.tile(g["L0_c"].T, (1, TT)), cols,
        row(a("dt_b")), row(a("out_b")), row(a("ln_g")), row(a("ln_beta")), sel,
        row(np.arange(E, 0, -1).astype(np.float32)), row(f("bs2")),
    ], axis=1)
    w1s = [np.concatenate([f("Ws1")[:, k * H:(k + 1) * H], f("Ws11")[:, k * H:(k + 1) * H],
                           hidden_cols(f("bs1")[k * H:(k + 1) * H]), hidden_cols(f("bs11")[k * H:(k + 1) * H])], axis=1)
           for k in range(SHARED)]
    w1r = [np.concatenate([f("W1")[e], f("W11")[e], hidden_cols(f("b1")[e]), hidden_cols(f("b11")[e])], axis=1)
           for e in range(E)]

    def second(w):
        return w.reshape(MH, P, D).transpose(1, 0, 2).reshape(P, MH * D)

    w2s = [second(f("Ws2")[k * H:(k + 1) * H]) for k in range(SHARED)] + [second(f("W2")[e]) for e in range(E)]
    nt = T // TT
    xt = a("x").reshape(B, nt, TT, D).transpose(2, 0, 1, 3).reshape(P, nt * D)
    arrays = {
        "in_x": xt, "in_wcol": wcol, "in_wmod": g["L0_wmod"], "in_w1": np.stack(w1s + w1r),
        "in_w2": np.stack(w2s), "in_b2": f("b2"),
    }
    arrays = {k: np.ascontiguousarray(v) for k, v in arrays.items()}
    nc = bacc.Bacc("TRN2", target_bir_lowering=False, num_devices=1)
    aps = {k: nc.dram_tensor(k, v.shape, mybir.dt.from_np(v.dtype), kind="ExternalInput").ap()
           for k, v in arrays.items()}
    out = nc.dram_tensor("out_0", (P, nt * D), F32, kind="ExternalOutput").ap()
    build(nc, aps["in_x"], aps["in_wcol"], aps["in_wmod"], aps["in_w1"], aps["in_w2"], aps["in_b2"], out)
    r = run_bass_kernel_spmd(nc, [arrays], core_ids=[0])
    y = r.results[0]["out_0"]
    return y.reshape(TT, B, nt, D).transpose(1, 2, 0, 3).reshape(B, T, D)
```
